# Optimizing a Trainium2 kernel written in Bass

```python
import numpy as np
import jax
import jax.numpy as jnp

def _softmax(x, axis=-1):
    return jax.nn.softmax(x, axis=axis)

def _gelu(x):
    return jax.nn.gelu(x, approximate=True)

def _silu(x):
    return jax.nn.silu(x)

def _sigmoid(x):
    return jax.nn.sigmoid(x)

def _layernorm(x, axis=-1, eps=1e-05):
    m = jnp.mean(x, axis=axis, keepdims=True)
    v = jnp.var(x, axis=axis, keepdims=True)
    return (x - m) / jnp.sqrt(v + eps)

def _scatter_add(tgt, idx, src, axis=0):
    return tgt.at[idx].add(src)

def _segment_sum(src, seg, n):
    return jax.ops.segment_sum(src, seg, n)
kernel_name = 'mk_dlrm_tower_d1_rec_r8_290ecc'

def setup_inputs(seed: int=0):
    np.random.seed(seed)
    _w = jnp.asarray

    def _rec_inputs():
        import jax
        import jax.numpy as jnp
        _tk = jax.random.key(seed)
        dense_ctx = jax.random.normal(jax.random.fold_in(_tk, 190), (2048, 16), jnp.float32)
        ids = jnp.stack([jax.random.randint(jax.random.fold_in(_tk, 200 + f), (2048,), 0, v, jnp.int32) for f, v in enumerate([125000, 12500, 1000, 1250, 12500, 1000, 1250, 12500, 1250, 12500, 1250, 1250, 1250, 125000, 1250, 12500, 12500, 125000, 12500, 1250, 1000, 12500, 1000, 125000, 12500, 125000, 12500, 1250, 12500, 1000, 125000, 125000])], axis=1)
        tbl_0 = 0.05 * jax.random.normal(jax.random.fold_in(_tk, 500 + 0), (125000, 16), jnp.float32)
        tbl_1 = 0.05 * jax.random.normal(jax.random.fold_in(_tk, 500 + 1), (12500, 16), jnp.float32)
        tbl_2 = 0.05 * jax.random.normal(jax.random.fold_in(_tk, 500 + 2), (1000, 16), jnp.float32)
        tbl_3 = 0.05 * jax.random.normal(jax.random.fold_in(_tk, 500 + 3), (1250, 16), jnp.float32)
        tbl_4 = 0.05 * jax.random.normal(jax.random.fold_in(_tk, 500 + 4), (12500, 16), jnp.float32)
        tbl_5 = 0.05 * jax.random.normal(jax.random.fold_in(_tk, 500 + 5), (1000, 16), jnp.float32)
        tbl_6 = 0.05 * jax.random.normal(jax.random.fold_in(_tk, 500 + 6), (1250, 16), jnp.float32)
        tbl_7 = 0.05 * jax.random.normal(jax.random.fold_in(_tk, 500 + 7), (12500, 16), jnp.float32)
        tbl_8 = 0.05 * jax.random.normal(jax.random.fold_in(_tk, 500 + 8), (1250, 16), jnp.float32)
        tbl_9 = 0.05 * jax.random.normal(jax.random.fold_in(_tk, 500 + 9), (12500, 16), jnp.float32)
        tbl_10 = 0.05 * jax.random.normal(jax.random.fold_in(_tk, 500 + 10), (1250, 16), jnp.float32)
        tbl_11 = 0.05 * jax.random.normal(jax.random.fold_in(_tk, 500 + 11), (1250, 16), jnp.float32)
        tbl_12 = 0.05 * jax.random.normal(jax.random.fold_in(_tk, 500 + 12), (1250, 16), jnp.float32)
        tbl_13 = 0.05 * jax.random.normal(jax.random.fold_in(_tk, 500 + 13), (125000, 16), jnp.float32)
        tbl_14 = 0.05 * jax.random.normal(jax.random.fold_in(_tk, 500 + 14), (1250, 16), jnp.float32)
        tbl_15 = 0.05 * jax.random.normal(jax.random.fold_in(_tk, 500 + 15), (12500, 16), jnp.float32)
        tbl_16 = 0.05 * jax.random.normal(jax.random.fold_in(_tk, 500 + 16), (12500, 16), jnp.float32)
        tbl_17 = 0.05 * jax.random.normal(jax.random.fold_in(_tk, 500 + 17), (125000, 16), jnp.float32)
        tbl_18 = 0.05 * jax.random.normal(jax.random.fold_in(_tk, 500 + 18), (12500, 16), jnp.float32)
        tbl_19 = 0.05 * jax.random.normal(jax.random.fold_in(_tk, 500 + 19), (1250, 16), jnp.float32)
        tbl_20 = 0.05 * jax.random.normal(jax.random.fold_in(_tk, 500 + 20), (1000, 16), jnp.float32)
        tbl_21 = 0.05 * jax.random.normal(jax.random.fold_in(_tk, 500 + 21), (12500, 16), jnp.float32)
        tbl_22 = 0.05 * jax.random.normal(jax.random.fold_in(_tk, 500 + 22), (1000, 16), jnp.float32)
        tbl_23 = 0.05 * jax.random.normal(jax.random.fold_in(_tk, 500 + 23), (125000, 16), jnp.float32)
        tbl_24 = 0.05 * jax.random.normal(jax.random.fold_in(_tk, 500 + 24), (12500, 16), jnp.float32)
        tbl_25 = 0.05 * jax.random.normal(jax.random.fold_in(_tk, 500 + 25), (125000, 16), jnp.float32)
        tbl_26 = 0.05 * jax.random.normal(jax.random.fold_in(_tk, 500 + 26), (12500, 16), jnp.float32)
        tbl_27 = 0.05 * jax.random.normal(jax.random.fold_in(_tk, 500 + 27), (1250, 16), jnp.float32)
        tbl_28 = 0.05 * jax.random.normal(jax.random.fold_in(_tk, 500 + 28), (12500, 16), jnp.float32)
        tbl_29 = 0.05 * jax.random.normal(jax.random.fold_in(_tk, 500 + 29), (1000, 16), jnp.float32)
        tbl_30 = 0.05 * jax.random.normal(jax.random.fold_in(_tk, 500 + 30), (125000, 16), jnp.float32)
        tbl_31 = 0.05 * jax.random.normal(jax.random.fold_in(_tk, 500 + 31), (125000, 16), jnp.float32)
        _rk = jax.random.fold_in(_tk, 7)
        W_top1 = 0.0693375 * jax.random.normal(jax.random.fold_in(_tk, 801), (208, 512), jnp.float32)
        W_top2 = 0.0441942 * jax.random.normal(jax.random.fold_in(_tk, 802), (512, 256), jnp.float32)
        W_top3 = 0.0625 * jax.random.normal(jax.random.fold_in(_tk, 803), (256, 1), jnp.float32)
        b_top1 = jnp.zeros((512,), jnp.float32)
        b_top2 = jnp.zeros((256,), jnp.float32)
        return (dense_ctx, ids, tbl_0, tbl_1, tbl_2, tbl_3, tbl_4, tbl_5, tbl_6, tbl_7, tbl_8, tbl_9, tbl_10, tbl_11, tbl_12, tbl_13, tbl_14, tbl_15, tbl_16, tbl_17, tbl_18, tbl_19, tbl_20, tbl_21, tbl_22, tbl_23, tbl_24, tbl_25, tbl_26, tbl_27, tbl_28, tbl_29, tbl_30, tbl_31, W_top1, b_top1, W_top2, b_top2, W_top3)
    dense_ctx, ids, tbl_0, tbl_1, tbl_2, tbl_3, tbl_4, tbl_5, tbl_6, tbl_7, tbl_8, tbl_9, tbl_10, tbl_11, tbl_12, tbl_13, tbl_14, tbl_15, tbl_16, tbl_17, tbl_18, tbl_19, tbl_20, tbl_21, tbl_22, tbl_23, tbl_24, tbl_25, tbl_26, tbl_27, tbl_28, tbl_29, tbl_30, tbl_31, W_top1, b_top1, W_top2, b_top2, W_top3 = _rec_inputs()

    def _L0_rec_setup():
        import jax, jax.numpy as jnp
        import numpy as np
        B, M, D = (2048, 32, 16)
        LAYERS = [64, 64, 64]
        key = jax.random.key(seed)
        ks = jax.random.split(key, 4)
        inp = {'embeddings': jax.random.normal(ks[0], (B, M, D), dtype=jnp.float32)}
        hk_1 = M
        for i, hk in enumerate(LAYERS):
            scale = (2.0 / (M * hk_1 + hk)) ** 0.5
            inp[f'W{i}'] = jax.random.normal(ks[i + 1], (M, hk_1, hk), dtype=jnp.float32) * scale
            hk_1 = hk
        return inp
    _L0_rec_all = _L0_rec_setup()
    _L0_rec_in = {k: v for k, v in _L0_rec_all.items() if k in ('W0', 'W1', 'W2')}
    del _L0_rec_all
    return {'dense_ctx': dense_ctx, 'ids': ids, 'tbl_0': tbl_0, 'tbl_1': tbl_1, 'tbl_2': tbl_2, 'tbl_3': tbl_3, 'tbl_4': tbl_4, 'tbl_5': tbl_5, 'tbl_6': tbl_6, 'tbl_7': tbl_7, 'tbl_8': tbl_8, 'tbl_9': tbl_9, 'tbl_10': tbl_10, 'tbl_11': tbl_11, 'tbl_12': tbl_12, 'tbl_13': tbl_13, 'tbl_14': tbl_14, 'tbl_15': tbl_15, 'tbl_16': tbl_16, 'tbl_17': tbl_17, 'tbl_18': tbl_18, 'tbl_19': tbl_19, 'tbl_20': tbl_20, 'tbl_21': tbl_21, 'tbl_22': tbl_22, 'tbl_23': tbl_23, 'tbl_24': tbl_24, 'tbl_25': tbl_25, 'tbl_26': tbl_26, 'tbl_27': tbl_27, 'tbl_28': tbl_28, 'tbl_29': tbl_29, 'tbl_30': tbl_30, 'tbl_31': tbl_31, 'W_top1': W_top1, 'b_top1': b_top1, 'W_top2': W_top2, 'b_top2': b_top2, 'W_top3': W_top3, 'L0_rec_W0': _L0_rec_in['W0'], 'L0_rec_W1': _L0_rec_in['W1'], 'L0_rec_W2': _L0_rec_in['W2']}

def reference(dense_ctx, ids, tbl_0, tbl_1, tbl_2, tbl_3, tbl_4, tbl_5, tbl_6, tbl_7, tbl_8, tbl_9, tbl_10, tbl_11, tbl_12, tbl_13, tbl_14, tbl_15, tbl_16, tbl_17, tbl_18, tbl_19, tbl_20, tbl_21, tbl_22, tbl_23, tbl_24, tbl_25, tbl_26, tbl_27, tbl_28, tbl_29, tbl_30, tbl_31, W_top1, b_top1, W_top2, b_top2, W_top3, L0_rec_W0, L0_rec_W1, L0_rec_W2):
    import jax
    import jax.numpy as jnp

    def _L0_rec_ref(embeddings, W0, W1, W2):
        import jax, jax.numpy as jnp
        import numpy as np
        B, M, D = (2048, 32, 16)
        LAYERS = [64, 64, 64]
        x0 = embeddings
        xk = x0
        outs = []
        for W in (W0, W1, W2):
            xk = jax.nn.relu(jnp.einsum('bmd,bhd,mhk->bkd', x0, xk, W))
            outs.append(jnp.sum(xk, axis=2))
        return jnp.concatenate(outs, axis=1)
    e = jnp.stack([tbl_0[ids[:, 0]], tbl_1[ids[:, 1]], tbl_2[ids[:, 2]], tbl_3[ids[:, 3]], tbl_4[ids[:, 4]], tbl_5[ids[:, 5]], tbl_6[ids[:, 6]], tbl_7[ids[:, 7]], tbl_8[ids[:, 8]], tbl_9[ids[:, 9]], tbl_10[ids[:, 10]], tbl_11[ids[:, 11]], tbl_12[ids[:, 12]], tbl_13[ids[:, 13]], tbl_14[ids[:, 14]], tbl_15[ids[:, 15]], tbl_16[ids[:, 16]], tbl_17[ids[:, 17]], tbl_18[ids[:, 18]], tbl_19[ids[:, 19]], tbl_20[ids[:, 20]], tbl_21[ids[:, 21]], tbl_22[ids[:, 22]], tbl_23[ids[:, 23]], tbl_24[ids[:, 24]], tbl_25[ids[:, 25]], tbl_26[ids[:, 26]], tbl_27[ids[:, 27]], tbl_28[ids[:, 28]], tbl_29[ids[:, 29]], tbl_30[ids[:, 30]], tbl_31[ids[:, 31]]], axis=1)
    z = _L0_rec_ref(e, L0_rec_W0, L0_rec_W1, L0_rec_W2)
    z = z.reshape(z.shape[0], -1)
    h = jnp.concatenate([z, dense_ctx], axis=1)
    h = jnp.maximum(h @ W_top1 + b_top1, 0.0)
    h = jnp.maximum(h @ W_top2 + b_top2, 0.0)
    y = h @ W_top3
    return y

_drawn_inputs = setup_inputs


def setup_inputs(seed=0):
    import zlib

    import numpy as np

    out = dict(_drawn_inputs(seed))
    spreads = {'b_top1': (0.0, 2.0), 'b_top2': (0.0, 0.8)}
    factors = {'tbl_0': 8.0,
     'tbl_1': 8.0,
     'tbl_2': 8.0,
     'tbl_3': 8.0,
     'tbl_4': 8.0,
     'tbl_5': 8.0,
     'tbl_6': 8.0,
     'tbl_7': 8.0,
     'tbl_8': 8.0,
     'tbl_9': 8.0,
     'tbl_10': 8.0,
     'tbl_11': 8.0,
     'tbl_12': 8.0,
     'tbl_13': 8.0,
     'tbl_14': 8.0,
     'tbl_15': 8.0,
     'tbl_16': 8.0,
     'tbl_17': 8.0,
     'tbl_18': 8.0,
     'tbl_19': 8.0,
     'tbl_20': 8.0,
     'tbl_21': 8.0,
     'tbl_22': 8.0,
     'tbl_23': 8.0,
     'tbl_24': 8.0,
     'tbl_25': 8.0,
     'tbl_26': 8.0,
     'tbl_27': 8.0,
     'tbl_28': 8.0,
     'tbl_29': 8.0,
     'tbl_30': 8.0,
     'tbl_31': 8.0,
     'L0_rec_W0': 3.481,
     'L0_rec_W1': 8.0,
     'L0_rec_W2': 8.0,
     'dense_ctx': 7.345}
    for name, (base, spread) in spreads.items():
        noise = np.random.default_rng([zlib.crc32(name.encode()), seed]).standard_normal(out[name].shape)
        drawn = base * np.exp(spread * noise) if base else spread * noise
        out[name] = jnp.asarray(drawn.astype(out[name].dtype))
    for name, factor in factors.items():
        out[name] = (out[name] * factor).astype(out[name].dtype)
    return out
```

```python
import concourse.bass as bass
from concourse import mybir
from contextlib import ExitStack

F32 = mybir.dt.float32
I32 = mybir.dt.int32
ALU = mybir.AluOpType
ACT = mybir.ActivationFunctionType
AX = mybir.AxisListType

P = 128
B, M, D, H = 2048, 32, 16, 64
NLAYER = 3
TILES = B // P
STEPS = 2 * TILES
CH = 512
DC = CH // P
COLS = 2 * CH
MT = M // 2
POOL_MT = 2
NSHIFT = M // 2
L0_MT = NSHIFT * M // P
GROUP = 4
SLOT_MT = 2
NSLOT = 4
L0_SLOTS = L0_MT // SLOT_MT
L12_SLOTS = (MT - POOL_MT) // SLOT_MT
STEP_SLOTS = 2 * L12_SLOTS + L0_SLOTS
GATHERS = (8, 12, 12)
GROUP_DMAS = GROUP * 2
F1, F2 = 512, 256
ZD = NLAYER * H


def following(i, p):
    return (i, 1) if p == 0 else (i + 1, 0)


def is_int(x, *values):
    return isinstance(x, int) and x in values


def slot_of(i, p, layer, k=0):
    s = 2 * i + p
    if layer == 0:
        return k if is_int(s, 0) else L0_SLOTS + (s - 1) * STEP_SLOTS + L12_SLOTS + k
    if layer == 1:
        return L0_SLOTS + s * STEP_SLOTS + k
    between = 0 if is_int(s, STEPS - 1) else L0_SLOTS
    return L0_SLOTS + s * STEP_SLOTS + L12_SLOTS + between + k


def run_of(i, p, layer):
    s = 2 * i + p
    if layer == 0:
        return 0 if is_int(s, 0) else 3 * s - 1
    return 3 * s + 1 if layer == 1 else (3 * s + 2 if is_int(s, STEPS - 1) else 3 * s + 3)


def some_tile(i):
    return i if isinstance(i, int) else 1


def slot_buffer(i, p, layer, k):
    return slot_of(some_tile(i), p, layer, k) % NSLOT


def run_parity(i, p, layer):
    return run_of(some_tile(i), p, layer) % 2


def pool_run(i, p, layer):
    return 2 * (2 * i + p) + layer - 1


def cin(nc, dense_t, ids, tables, w_top1, b_top1, w_top2, b_top2, w_top3, w0_pair, w0_swap, w0_diag,
        w1, w2, out):
    ctx = ExitStack()
    with ctx:
        def sb(name, shape, dt=F32):
            return ctx.enter_context(nc.sbuf_tensor(name, shape, dt))

        def sem(name):
            return ctx.enter_context(nc.semaphore(name))

        ident = sb("ident", [P, P])
        ids_sb = sb("ids_sb", [P, M], I32)
        emb = sb("emb", [P, M, D])
        x0t = [sb(f"x0t{p}", [P, COLS]) for p in range(2)]
        squares = sb("squares", [M, COLS])
        shifted = sb("shifted", [P, L0_MT, COLS])
        rep0 = [sb(f"rep0_{p}", [P, GROUP, COLS]) for p in range(2)]
        rep123 = sb("rep123", [P, MT - GROUP, COLS])
        slots = [sb(f"slot{n}", [P, 2, SLOT_MT, CH]) for n in range(NSLOT)]
        pool_prod = sb("pool_prod", [P, 2, POOL_MT, CH])
        x_pool = [sb(f"x_pool{p}", [P, 2, CH]) for p in range(2)]
        stacked = [sb(f"stacked{p}", [P, CH]) for p in range(2)]
        zhalf = [sb(f"zhalf{p}", [P, NLAYER, P]) for p in range(2)]
        z = sb("z", [P, NLAYER, B])
        w0_sb = sb("w0_sb", [P, L0_MT, H])
        wd_sb = sb("wd_sb", [M, H])
        w12_sb = [sb(f"w{n}_sb", [P, MT, H]) for n in (1, 2)]
        b1_sb = sb("b1_sb", [P, F1 // P])
        b2_sb = sb("b2_sb", [P, F2 // P])
        w0_swap_sb = pool_prod[:, 0, 0, 0:L0_MT * H].rearrange("p (j k) -> p j k", j=L0_MT)

        sh = shifted[:, :, :].rearrange("p a b -> p (a b)")
        wt1_z = sh[:, 0:NLAYER * F1].rearrange("p (l n) -> p l n", l=NLAYER)
        wt1_d = sh[0:D, NLAYER * F1:(NLAYER + 1) * F1]
        wt2 = sh[:, 4 * F1:4 * F1 + 4 * F2].rearrange("p (t n) -> p t n", t=F1 // P)
        wt3 = sh[:, 4 * F1 + 4 * F2:4 * F1 + 4 * F2 + F2 // P]
        dense_sb = [x0t[0][0:D, :], x0t[1][0:D, :]]
        h1 = rep123[:, 0:8, :].rearrange("p a b -> p (a b)").rearrange("p (t n) -> p t n", t=F1 // P)
        h2 = rep0[0][:, :, :].rearrange("p a b -> p (a b)").rearrange("p (t n) -> p t n", t=F2 // P)
        y_sb = rep0[1][0:1, 0:2, :].rearrange("p a b -> p (a b)")

        acc = [ctx.enter_context(nc.psum_tensor(f"acc{n}", [P, CH], F32)) for n in range(2)]
        x_ps = [ctx.enter_context(nc.psum_tensor(f"x_ps{n}", [P, 2, CH], F32)) for n in range(2)]
        tr = ctx.enter_context(nc.psum_tensor("tr", [P, 2, CH], F32))

        weights_in = sem("weights_in")
        w0_summed = sem("w0_summed")
        ident_made = sem("ident_made")
        ids_in = sem("ids_in")
        gathered = sem("gathered")
        transposed = sem("transposed")
        x0_ready = sem("x0_ready")
        shifted_in = sem("shifted_in")
        rep0_in = [sem(f"rep0_in{p}") for p in range(2)]
        rep_in = [None] + [sem(f"rep{g}_in") for g in (1, 2, 3)]
        slot_full = sem("slot_full")
        slot_used = sem("slot_used")
        pool_full = sem("pool_full")
        pool_used = sem("pool_used")
        acc_used = sem("acc_used")
        x_ready = sem("x_ready")
        x_pool_ready = sem("x_pool_ready")
        summed = sem("summed")
        z_ready = sem("z_ready")
        mlp_in = sem("mlp_in")
        mlp_full = sem("mlp_full")
        mlp_out = sem("mlp_out")
        y_stored = sem("y_stored")

        mlp_banks = [acc[0][:, :], acc[1][:, :], tr[:, 0, :], tr[:, 1, :]]
        block = ctx.enter_context(nc.Block())

        def rep_tiles(p, t0, n):
            if t0 < GROUP:
                return rep0[p][:, t0:t0 + n, :]
            return rep123[:, t0 - GROUP:t0 - GROUP + n, :]

        @block.sync
        def _(sp):
            def load_ids(i):
                sp.dma_start(ids_sb[:, :], ids[bass.ts(i, P), :]).then_inc(ids_in, 16)

            def load_shifted(p):
                for j in range(L0_MT):
                    for g in range(P // M):
                        q = P // M * j + g + 1 + (P // 2 if g % 2 else 0)
                        sp.dma_start(shifted[M * g:M * g + M, j, :], x0t[p][q:q + M, :])\
                            .then_inc(shifted_in, 16)

            def load_group(p, g, signal):
                for m in range(2 * GROUP * g, 2 * GROUP * (g + 1)):
                    lo = H * (m % 2)
                    src = x0t[p][lo + m % M:lo + m % M + 1, :]
                    sp.dma_start(rep_tiles(p, m // 2, 1)[lo:lo + H, 0, :],
                                 src.unsqueeze(1).broadcast_to([1, H, COLS])).then_inc(signal, 16)

            def load_groups123(i, p, before):
                for g in (1, 2, 3):
                    sp.wait_ge(slot_full, slot_of(*before, 2, 2 * g) + 1)
                    load_group(p, g, rep_in[g])

            load_ids(0)
            sp.dma_start(w0_sb[:, :, :], w0_pair).then_inc(weights_in, 16)
            sp.dma_start(w0_swap_sb, w0_swap).then_inc(weights_in, 16)
            sp.dma_start(wd_sb[:, :], w0_diag).then_inc(weights_in, 16)
            for n, w in enumerate((w1, w2)):
                sp.dma_start(w12_sb[n][:, :, :], w.rearrange("(t a) h k -> (a h) t k", a=2))\
                    .then_inc(weights_in, 16)
            sp.dma_start(b1_sb[:, :], b_top1.rearrange("(t p) -> p t", p=P),
                         allow_slow_non_contiguous=True).then_inc(weights_in, 16)
            sp.dma_start(b2_sb[:, :], b_top2.rearrange("(t p) -> p t", p=P),
                         allow_slow_non_contiguous=True).then_inc(weights_in, 16)
            sp.wait_ge(x0_ready, 1)
            load_shifted(0)
            load_group(0, 0, rep0_in[0])
            for g in (1, 2, 3):
                load_group(0, g, rep_in[g])
            sp.wait_ge(gathered, 16 * M)
            load_ids(1)
            sp.wait_ge(x0_ready, 2)
            sp.wait_ge(shifted_in, 16 * NSHIFT)
            sp.wait_ge(slot_full, slot_of(0, 0, 0) + L0_SLOTS)
            load_shifted(1)
            load_group(1, 0, rep0_in[1])

            def turn(i, more_ids=True, last=False):
                load_groups123(i, 1, (i, 0))
                if last:
                    return
                sp.wait_ge(x0_ready, 2 * i + 3)
                load_shifted(0)
                sp.wait_ge(pool_full, pool_run(i, 0, 2) + 1)
                load_group(0, 0, rep0_in[0])
                sp.wait_ge(x0_ready, 2 * i + 4)
                sp.wait_ge(gathered, 16 * M * (i + 2))
                sp.wait_ge(slot_full, slot_of(i + 1, 0, 0) + L0_SLOTS)
                load_shifted(1)
                if more_ids:
                    load_ids(i + 2)
                load_groups123(i + 1, 0, (i, 1))
                sp.wait_ge(pool_full, pool_run(i, 1, 2) + 1)
                load_group(1, 0, rep0_in[1])

            turn(0)
            with sp.Fori(1, TILES - 2) as i:
                turn(i)
            turn(TILES - 2, more_ids=False)
            turn(TILES - 1, last=True)

            for half in range(2):
                sp.dma_start(wt1_z[H * half:H * half + H, :, :],
                             w_top1[0:ZD, :].rearrange("(l k) n -> k l n", k=H)).then_inc(mlp_in, 16)
            sp.dma_start(wt1_d, w_top1[ZD:ZD + D, :]).then_inc(mlp_in, 16)
            sp.dma_start(wt2, w_top2.rearrange("(t p) n -> p t n", p=P)).then_inc(mlp_in, 16)
            sp.dma_start(wt3, w_top3.rearrange("(t p) o -> p (t o)", p=P),
                         allow_slow_non_contiguous=True).then_inc(mlp_in, 16)
            for g in (1, 2, 3):
                sp.wait_ge(rep_in[g], 16 * GROUP_DMAS * STEPS)
            for n in range(2):
                sp.wait_ge(rep0_in[n], 16 * GROUP_DMAS * TILES)
                sp.dma_start(dense_sb[n], dense_t[:, COLS * n:COLS * (n + 1)]).then_inc(mlp_in, 16)
            sp.wait_ge(mlp_out, (B // CH) * (F1 // P + F2 // P + 1))
            sp.dma_start(out.rearrange("b o -> o b"), y_sb).then_inc(y_stored, 16)
            sp.wait_ge(y_stored, 16)

        @block.gpsimd
        def _(pool):
            def gather(first, n):
                for m in range(first, first + n):
                    nc.gpsimd.indirect_dma_start(
                        emb[:, m, :], None, tables[m][:, :],
                        bass.IndirectOffsetOnAxis(ap=ids_sb[:, m:m + 1], axis=0),
                    ).then_inc(gathered, 16)

            pool.wait_ge(ids_in, 16)
            gather(0, M)
            nc.gpsimd.memset(ident[:, :], 0.0).then_inc(ident_made, 1)
            pool.wait_ge(ident_made, 1)
            nc.gpsimd.affine_select(out=ident[:, :], in_=ident[:, :], compare_op=ALU.not_equal, fill=1.0,
                                    base=0, pattern=[[-1, P]], channel_multiplier=1).then_inc(ident_made, 1)
            pool.wait_ge(w0_summed, 1)

            def products(i, p, layer):
                run = pool_run(i, p, layer)
                if layer == 1:
                    pool.wait_ge(rep0_in[p], (i + 1) * 16 * GROUP_DMAS)
                pool.wait_ge(x_pool_ready, run + 1)
                if not is_int(run, 0):
                    pool.wait_ge(pool_used, run)
                nc.gpsimd.tensor_tensor(
                    pool_prod[:, :, :, :],
                    x_pool[p][:, :, :].unsqueeze(2).broadcast_to([P, 2, POOL_MT, CH]),
                    rep_tiles(p, 0, POOL_MT).rearrange("p t (c n) -> p c t n", c=2),
                    ALU.mult).then_inc(pool_full, 1)

            def turn(i, last=False):
                if not last:
                    gather(0, GATHERS[0])
                products(i, 0, 1)
                if not last:
                    gather(GATHERS[0], GATHERS[1])
                products(i, 0, 2)
                if not last:
                    gather(GATHERS[0] + GATHERS[1], GATHERS[2])
                products(i, 1, 1)

            def may_gather(i):
                pool.wait_ge(ids_in, 16 * (i + 2))
                pool.wait_ge(transposed, 2 * i + 2)

            may_gather(0)
            turn(0)
            with pool.Fori(1, TILES - 1) as i:
                may_gather(i)
                products(i - 1, 1, 2)
                turn(i)
            products(TILES - 2, 1, 2)
            turn(TILES - 1, last=True)
            products(TILES - 1, 1, 2)

        @block.vector
        def _(dve):
            def product(i, p, layer, k, x, x0):
                n = slot_of(i, p, layer, k)
                if not is_int(n, *range(NSLOT)):
                    dve.wait_ge(slot_used, n - NSLOT + 1)
                nc.vector.tensor_tensor(slots[slot_buffer(i, p, layer, k)][:, :, :, :],
                                        x.unsqueeze(2).broadcast_to([P, 2, SLOT_MT, CH]),
                                        x0.rearrange("p t (c n) -> p c t n", c=2),
                                        ALU.mult).then_inc(slot_full, 1)

            def layer0(i, p):
                s = 2 * i + p
                dve.wait_ge(x0_ready, s + 1)
                dve.wait_ge(shifted_in, 16 * NSHIFT * (s + 1))
                for k in range(L0_SLOTS):
                    product(i, p, 0, k, x0t[p][:, :].rearrange("p (c n) -> p c n", c=2),
                            shifted[:, SLOT_MT * k:SLOT_MT * (k + 1), :])

            def layer12(i, p, layer, ks):
                for k in ks:
                    t = POOL_MT + SLOT_MT * k
                    if k == 0:
                        dve.wait_ge(x_ready, 2 * (2 * i + p) + layer)
                        if layer == 1:
                            dve.wait_ge(rep0_in[p], (i + 1) * 16 * GROUP_DMAS)
                    if layer == 1 and t % GROUP == 0:
                        dve.wait_ge(rep_in[t // GROUP], (2 * i + p + 1) * 16 * GROUP_DMAS)
                    product(i, p, layer, k, x_ps[p][:, :, :], rep_tiles(p, t, SLOT_MT))

            def sum_over_d(i, p, layer):
                run = run_of(i, p, layer)
                dve.wait_ge(acc_used, run + 1)
                nc.vector.tensor_reduce(zhalf[p][:, layer, :],
                                        stacked[run_parity(i, p, layer)][:, :].rearrange("p (d b) -> p b d", d=DC),
                                        AX.X, ALU.add).then_inc(summed, 1)
                if p == 1:
                    dve.wait_ge(summed, run + 1)
                    nc.vector.tensor_tensor(z[:, layer, bass.ts(i, P)], zhalf[0][:, layer, :],
                                            zhalf[1][:, layer, :], ALU.add).then_inc(z_ready, 1)

            dve.wait_ge(weights_in, 16 * 7)
            nc.vector.tensor_tensor(w0_sb[:, 0:L0_MT - 1, :], w0_sb[:, 0:L0_MT - 1, :],
                                    w0_swap_sb[:, 0:L0_MT - 1, :], ALU.add)
            nc.vector.tensor_tensor(w0_sb[0:P - M, L0_MT - 1, :], w0_sb[0:P - M, L0_MT - 1, :],
                                    w0_swap_sb[0:P - M, L0_MT - 1, :], ALU.add).then_inc(w0_summed, 1)
            layer0(0, 0)
            sum_over_d(0, 0, 0)

            def turn(i, first=False, last=False):
                for p in range(2):
                    more = not (last and p == 1)
                    layer12(i, p, 1, range(0, 3))
                    if not (first and p == 0):
                        sum_over_d(*((i - 1, 1) if p == 0 else (i, 0)), 2)
                    layer12(i, p, 1, range(3, L12_SLOTS))
                    if more:
                        layer0(*following(i, p))
                    layer12(i, p, 2, range(0, 2))
                    sum_over_d(i, p, 1)
                    layer12(i, p, 2, range(2, 4))
                    if more:
                        sum_over_d(*following(i, p), 0)
                    layer12(i, p, 2, range(4, L12_SLOTS))

            turn(0, first=True)
            with dve.Fori(1, TILES - 1) as i:
                turn(i)
            turn(TILES - 1, last=True)
            sum_over_d(TILES - 1, 1, 2)

        @block.tensor
        def _(pe):
            def transpose(i, p):
                s = 2 * i + p
                if p == 0:
                    pe.wait_ge(gathered, 16 * M * (i + 1))
                if not is_int(s, 0):
                    pe.wait_ge(x0_ready, s)
                for c in range(2):
                    for d in range(DC):
                        last = nc.tensor.transpose(tr[0:M, c, P * d:P * (d + 1)],
                                                   emb[:, :, (2 * p + c) * DC + d], ident[:, :])
                last.then_inc(transposed, 1)

            def pair_tile(bank, weight, moving, start, stop):
                for c in range(2):
                    last = nc.tensor.matmul(bank[H * c:H * c + H, :], weight, moving[:, c, :],
                                            start=start, stop=stop)
                return last

            def take_bank(i, p, layer):
                run = run_of(i, p, layer)
                if not is_int(run, 0, 1):
                    pe.wait_ge(acc_used, run - 1)
                return acc[run_parity(i, p, layer)]

            def from_slots(i, p, layer, bank, weights, first, n_slots):
                for k in range(n_slots):
                    pe.wait_ge(slot_full, slot_of(i, p, layer, k) + 1)
                    for j in range(SLOT_MT):
                        last = pair_tile(bank, weights[:, first + SLOT_MT * k + j, :],
                                         slots[slot_buffer(i, p, layer, k)][:, :, j, :],
                                         start=layer > 0 and (k, j) == (0, 0),
                                         stop=layer == 0 and (k, j) == (n_slots - 1, SLOT_MT - 1))
                    last.then_inc(slot_used, 1)

            def layer0(i, p):
                bank = take_bank(i, p, 0)
                pe.wait_ge(x0_ready, 2 * i + p + 1)
                pair_tile(bank, wd_sb[:, :], squares[:, :].rearrange("p (c n) -> p c n", c=2), True, False)
                from_slots(i, p, 0, bank, w0_sb, 0, L0_SLOTS)

            def layer12(i, p, layer):
                bank = take_bank(i, p, layer)
                weights = w12_sb[layer - 1]
                from_slots(i, p, layer, bank, weights, POOL_MT, L12_SLOTS)
                pe.wait_ge(pool_full, pool_run(i, p, layer) + 1)
                for t in range(POOL_MT):
                    last = pair_tile(bank, weights[:, t, :], pool_prod[:, :, t, :], False, t == POOL_MT - 1)
                last.then_inc(pool_used, 1)

            pe.wait_ge(weights_in, 16 * 7)
            pe.wait_ge(ident_made, 2)
            pe.wait_ge(w0_summed, 1)
            transpose(0, 0)
            layer0(0, 0)
            transpose(0, 1)

            def turn(i, last=False):
                layer12(i, 0, 1)
                layer0(i, 1)
                layer12(i, 0, 2)
                if not last:
                    transpose(i + 1, 0)
                layer12(i, 1, 1)
                if not last:
                    layer0(i + 1, 0)
                    transpose(i + 1, 1)
                layer12(i, 1, 2)

            turn(0)
            with pe.Fori(1, TILES - 1) as i:
                turn(i)
            turn(TILES - 1, last=True)

            pe.wait_ge(mlp_in, 16 * 7)
            pe.wait_ge(z_ready, NLAYER * TILES)
            pe.wait_ge(acc_used, NLAYER * STEPS)
            u = 0
            for n in range(B // CH):
                cols = slice(CH * n, CH * (n + 1))
                dense = dense_sb[n // 2][:, CH * (n % 2):CH * (n % 2 + 1)]
                for t in range(F1 // P):
                    if u >= 4:
                        pe.wait_ge(mlp_out, u - 3)
                    for l in range(NLAYER):
                        nc.tensor.matmul(mlp_banks[u % 4], wt1_z[:, l, P * t:P * (t + 1)], z[:, l, cols],
                                         start=(l == 0), stop=False)
                    nc.tensor.matmul(mlp_banks[u % 4], wt1_d[:, P * t:P * (t + 1)], dense,
                                     start=False, stop=True).then_inc(mlp_full, 1)
                    u += 1
            for n in range(B // CH):
                cols = slice(CH * n, CH * (n + 1))
                for t in range(F2 // P):
                    pe.wait_ge(mlp_out, max(u - 3, (n + 1) * (F1 // P)))
                    for q in range(F1 // P):
                        last = nc.tensor.matmul(mlp_banks[u % 4], wt2[:, q, P * t:P * (t + 1)], h1[:, q, cols],
                                                start=(q == 0), stop=(q == F1 // P - 1))
                    last.then_inc(mlp_full, 1)
                    u += 1
            for n in range(B // CH):
                cols = slice(CH * n, CH * (n + 1))
                pe.wait_ge(mlp_out, max(u - 3, (B // CH) * (F1 // P) + (n + 1) * (F2 // P)))
                for q in range(F2 // P):
                    last = nc.tensor.matmul(mlp_banks[u % 4][0:1, :], wt3[:, q:q + 1], h2[:, q, cols],
                                            start=(q == 0), stop=(q == F2 // P - 1))
                last.then_inc(mlp_full, 1)
                u += 1

        @block.scalar
        def _(act):
            def take_x0(i, p):
                s = 2 * i + p
                act.wait_ge(transposed, s + 1)
                if not is_int(i, 0):
                    act.wait_ge(rep0_in[p], i * 16 * GROUP_DMAS)
                    for g in (1, 2, 3):
                        act.wait_ge(rep_in[g], (s - 1) * 16 * GROUP_DMAS)
                for g in range(P // M):
                    nc.scalar.activation(x0t[p][M * g:M * g + M, :].rearrange("p (c n) -> p c n", c=2),
                                         tr[0:M, :, :], ACT.Copy)
                nc.scalar.activation(squares[:, :].rearrange("p (c n) -> p c n", c=2), tr[0:M, :, :],
                                     ACT.Square).then_inc(x0_ready, 1)

            def finish(i, p, layer):
                run = run_of(i, p, layer)
                bank = acc[run_parity(i, p, layer)]
                if layer == 0:
                    act.wait_ge(slot_used, slot_of(i, p, 0) + L0_SLOTS)
                else:
                    act.wait_ge(pool_used, pool_run(i, p, layer) + 1)
                def both_halves(x):
                    for c in range(2):
                        for half in range(2):
                            last = nc.scalar.activation(x[H * half:H * half + H, c, :],
                                                        bank[H * c:H * c + H, :], ACT.Relu)
                    return last

                if layer < 2:
                    both_halves(x_ps[p]).then_inc(x_ready, 1)
                    if layer == 1:
                        act.wait_ge(pool_full, pool_run(i, p, 1) + 1)
                    elif not is_int(i, 0):
                        act.wait_ge(pool_full, pool_run(i - 1, p, 2) + 1)
                    both_halves(x_pool[p]).then_inc(x_pool_ready, 1)
                if not is_int(run, 0, 1):
                    act.wait_ge(summed, run - 1)
                nc.scalar.activation(stacked[run_parity(i, p, layer)][:, :], bank[:, :], ACT.Relu)\
                    .then_inc(acc_used, 1)

            take_x0(0, 0)
            finish(0, 0, 0)
            take_x0(0, 1)

            def turn(i, last=False):
                finish(i, 0, 1)
                finish(i, 1, 0)
                finish(i, 0, 2)
                if not last:
                    take_x0(i + 1, 0)
                finish(i, 1, 1)
                if not last:
                    finish(i + 1, 0, 0)
                    take_x0(i + 1, 1)
                finish(i, 1, 2)

            turn(0)
            with act.Fori(1, TILES - 1) as i:
                turn(i)
            turn(TILES - 1, last=True)

            act.wait_ge(weights_in, 16 * 7)
            act.wait_ge(slot_full, slot_of(TILES - 1, 1, 2) + L12_SLOTS)
            act.wait_ge(pool_full, pool_run(TILES - 1, 1, 2) + 1)
            u = 0
            for bias, hidden, width in ((b1_sb, h1, F1), (b2_sb, h2, F2)):
                for n in range(B // CH):
                    for t in range(width // P):
                        act.wait_ge(mlp_full, u + 1)
                        nc.scalar.activation(hidden[:, t, CH * n:CH * (n + 1)], mlp_banks[u % 4], ACT.Relu,
                                             bias=bias[:, t:t + 1]).then_inc(mlp_out, 1)
                        u += 1
            for n in range(B // CH):
                act.wait_ge(mlp_full, u + 1)
                nc.scalar.activation(y_sb[:, CH * n:CH * (n + 1)], mlp_banks[u % 4][0:1, :], ACT.Copy)\
                    .then_inc(mlp_out, 1)
                u += 1


def kernel(**inputs):
    import numpy as np
    import concourse.bacc as bacc
    from concourse import mybir as mb
    from concourse.bass_utils import run_bass_kernel_spmd

    w0 = np.asarray(inputs["L0_rec_W0"])
    m = np.arange(M)[None, :, None]
    shift = (np.arange(P // M)[:, None, None] + 1) + P // M * np.arange(L0_MT)[None, None, :]
    h = (m + shift) % M
    m = np.broadcast_to(m, h.shape)
    named = {
        "dense_t": np.ascontiguousarray(np.asarray(inputs["dense_ctx"]).T),
        "ids": np.ascontiguousarray(inputs["ids"]),
        **{f"tbl_{n}": np.ascontiguousarray(inputs[f"tbl_{n}"]) for n in range(M)},
        **{k: np.ascontiguousarray(inputs[k]) for k in ("W_top1", "b_top1", "W_top2", "b_top2", "W_top3")},
        "w0_pair": np.ascontiguousarray(w0[m, h].reshape(P, L0_MT, H)),
        "w0_swap": np.ascontiguousarray(w0[h, m].reshape(P, L0_MT, H)),
        "w0_diag": np.ascontiguousarray(w0[np.arange(M), np.arange(M)]),
        "W1": np.ascontiguousarray(inputs["L0_rec_W1"]),
        "W2": np.ascontiguousarray(inputs["L0_rec_W2"]),
    }
    nc = bacc.Bacc("TRN2", target_bir_lowering=False, num_devices=1)
    args = {k: nc.dram_tensor(f"in_{k}", a.shape, mb.dt.from_np(a.dtype), kind="ExternalInput").ap()
            for k, a in named.items()}
    out = nc.dram_tensor("out_y", (B, 1), mb.dt.float32, kind="ExternalOutput").ap()
    cin(nc, args["dense_t"], args["ids"], [args[f"tbl_{n}"] for n in range(M)], args["W_top1"],
        args["b_top1"], args["W_top2"], args["b_top2"], args["W_top3"], args["w0_pair"], args["w0_swap"],
        args["w0_diag"], args["W1"], args["W2"], out)
    r = run_bass_kernel_spmd(nc, [{f"in_{k}": a for k, a in named.items()}], core_ids=[0])
    return r.results[0]["out_y"]
```

```python
import concourse.bass as bass
from concourse import mybir
from contextlib import ExitStack

F32 = mybir.dt.float32
I32 = mybir.dt.int32
ALU = mybir.AluOpType
ACT = mybir.ActivationFunctionType
AX = mybir.AxisListType

P = 128
B, M, D, H = 2048, 32, 16, 64
NLAYER = 3
TILES = B // P
STEPS = 2 * TILES
CH = 512
DC = CH // P
COLS = 2 * CH
MT = M // 2
POOL_MT = 2
NSHIFT = M // 2
L0_MT = NSHIFT * M // P
GROUP = 4
SLOT_MT = 2
NSLOT = 4
L0_SLOTS = L0_MT // SLOT_MT
L12_SLOTS = (MT - POOL_MT) // SLOT_MT
STEP_SLOTS = 2 * L12_SLOTS + L0_SLOTS
TURNS = range(1, TILES // 2 - 2)
TR_SLOT = 4
GROUP_DMAS = GROUP * 2
F1, F2 = 512, 256
ZD = NLAYER * H


def following(i, p):
    return (i, 1) if p == 0 else (i + 1, 0)


def is_int(x, *values):
    return isinstance(x, int) and x in values


def slot_of(i, p, layer, k=0):
    s = 2 * i + p
    if layer == 0:
        return k if is_int(s, 0) else L0_SLOTS + (s - 1) * STEP_SLOTS + L12_SLOTS + k
    if layer == 1:
        return L0_SLOTS + s * STEP_SLOTS + k
    between = 0 if is_int(s, STEPS - 1) else L0_SLOTS
    return L0_SLOTS + s * STEP_SLOTS + L12_SLOTS + between + k


def run_of(i, p, layer):
    s = 2 * i + p
    if layer == 0:
        return 0 if is_int(s, 0) else 3 * s - 1
    return 3 * s + 1 if layer == 1 else (3 * s + 2 if is_int(s, STEPS - 1) else 3 * s + 3)


def exists(i):
    return not isinstance(i, int) or i < TILES


def gathered_count(i, q):
    return 16 * M // 2 * (i - q + 2)


def all_turns(engine, tile):
    for i in range(2 * TURNS.start):
        tile(i, i % 2)
    with engine.Fori(TURNS.start, TURNS.stop) as j:
        for q in range(2):
            tile(2 * j + q, q)
    for i in range(2 * TURNS.stop, TILES):
        tile(i, i % 2)


def some_tile(i):
    return i if isinstance(i, int) else 1


def slot_buffer(i, p, layer, k):
    return slot_of(some_tile(i), p, layer, k) % NSLOT


def run_parity(i, p, layer):
    return run_of(some_tile(i), p, layer) % 2


def pool_run(i, p, layer):
    return 2 * (2 * i + p) + layer - 1


def cin(nc, dense_t, ids, tables, w_top1, b_top1, w_top2, b_top2, w_top3, w0_pair, w0_swap, w0_diag,
        w1, w2, out):
    ctx = ExitStack()
    with ctx:
        def sb(name, shape, dt=F32):
            return ctx.enter_context(nc.sbuf_tensor(name, shape, dt))

        def sem(name):
            return ctx.enter_context(nc.semaphore(name))

        ident = sb("ident", [P, P])
        ids_sb = [sb(f"ids_sb{q}", [P, M], I32) for q in range(2)]
        emb = [sb(f"emb{q}", [P, M, D]) for q in range(2)]
        x0t = [sb(f"x0t{p}", [P, COLS]) for p in range(2)]
        squares = [sb(f"squares{p}", [M, COLS]) for p in range(2)]
        shifted = sb("shifted", [P, L0_MT, COLS])
        rep0 = [sb(f"rep0_{p}", [P, GROUP, COLS]) for p in range(2)]
        rep123 = sb("rep123", [P, MT - GROUP, COLS])
        slots = [sb(f"slot{n}", [P, 2, SLOT_MT, CH]) for n in range(NSLOT)]
        pool_prod = sb("pool_prod", [P, 2, POOL_MT, CH])
        x_pool = [sb(f"x_pool{p}", [P, 2, CH]) for p in range(2)]
        stacked = [sb(f"stacked{p}", [P, CH]) for p in range(2)]
        zhalf = [sb(f"zhalf{p}", [P, NLAYER, P]) for p in range(2)]
        z = sb("z", [P, NLAYER, B])
        w0_sb = sb("w0_sb", [P, L0_MT, H])
        wd_sb = sb("wd_sb", [M, H])
        w12_sb = [sb(f"w{n}_sb", [P, MT, H]) for n in (1, 2)]
        b1_sb = sb("b1_sb", [P, F1 // P])
        b2_sb = sb("b2_sb", [P, F2 // P])
        w0_swap_sb = pool_prod[:, 0, 0, 0:L0_MT * H].rearrange("p (j k) -> p j k", j=L0_MT)

        sh = shifted[:, :, :].rearrange("p a b -> p (a b)")
        wt1_z = sh[:, 0:NLAYER * F1].rearrange("p (l n) -> p l n", l=NLAYER)
        wt1_d = sh[0:D, NLAYER * F1:(NLAYER + 1) * F1]
        wt2 = sh[:, 4 * F1:4 * F1 + 4 * F2].rearrange("p (t n) -> p t n", t=F1 // P)
        wt3 = sh[:, 4 * F1 + 4 * F2:4 * F1 + 4 * F2 + F2 // P]
        dense_sb = [x0t[0][0:D, :], x0t[1][0:D, :]]
        h1 = rep123[:, 0:8, :].rearrange("p a b -> p (a b)").rearrange("p (t n) -> p t n", t=F1 // P)
        h2 = rep0[0][:, :, :].rearrange("p a b -> p (a b)").rearrange("p (t n) -> p t n", t=F2 // P)
        y_sb = rep0[1][0:1, 0:2, :].rearrange("p a b -> p (a b)")

        acc = [ctx.enter_context(nc.psum_tensor(f"acc{n}", [P, CH], F32)) for n in range(2)]
        x_ps = [ctx.enter_context(nc.psum_tensor(f"x_ps{n}", [P, 2, CH], F32)) for n in range(2)]
        tr = ctx.enter_context(nc.psum_tensor("tr", [P, 2, CH], F32))

        weights_in = sem("weights_in")
        w0_summed = sem("w0_summed")
        ident_made = sem("ident_made")
        ids_in = sem("ids_in")
        gathered = [sem(f"gathered{q}") for q in range(2)]
        transposed = sem("transposed")
        x0_ready = sem("x0_ready")
        shifted_in = sem("shifted_in")
        rep0_in = [sem(f"rep0_in{p}") for p in range(2)]
        rep_in = [None] + [sem(f"rep{g}_in") for g in (1, 2, 3)]
        slot_full = sem("slot_full")
        slot_used = sem("slot_used")
        pool_full = sem("pool_full")
        pool_used = sem("pool_used")
        acc_used = sem("acc_used")
        x_ready = sem("x_ready")
        x_pool_ready = sem("x_pool_ready")
        summed = sem("summed")
        z_ready = sem("z_ready")
        mlp_in = sem("mlp_in")
        mlp_full = sem("mlp_full")
        mlp_out = sem("mlp_out")
        y_stored = sem("y_stored")

        mlp_banks = [acc[0][:, :], acc[1][:, :], tr[:, 0, :], tr[:, 1, :]]
        block = ctx.enter_context(nc.Block())

        def rep_tiles(p, t0, n):
            if t0 < GROUP:
                return rep0[p][:, t0:t0 + n, :]
            return rep123[:, t0 - GROUP:t0 - GROUP + n, :]

        @block.sync
        def _(sp):
            def load_ids(i, q):
                sp.dma_start(ids_sb[q][:, :], ids[bass.ts(i, P), :]).then_inc(ids_in, 16)

            def load_shifted(p):
                for j in range(L0_MT):
                    for g in range(P // M):
                        q = P // M * j + g + 1 + (P // 2 if g % 2 else 0)
                        sp.dma_start(shifted[M * g:M * g + M, j, :], x0t[p][q:q + M, :])\
                            .then_inc(shifted_in, 16)

            def load_group(p, g, signal):
                for m in range(2 * GROUP * g, 2 * GROUP * (g + 1)):
                    lo = H * (m % 2)
                    src = x0t[p][lo + m % M:lo + m % M + 1, :]
                    sp.dma_start(rep_tiles(p, m // 2, 1)[lo:lo + H, 0, :],
                                 src.unsqueeze(1).broadcast_to([1, H, COLS])).then_inc(signal, 16)

            def load_groups123(i, p, before):
                for g in (1, 2, 3):
                    sp.wait_ge(slot_full, slot_of(*before, 2, 2 * g) + 1)
                    load_group(p, g, rep_in[g])

            load_ids(0, 0)
            load_ids(1, 1)
            sp.dma_start(w0_sb[:, :, :], w0_pair).then_inc(weights_in, 16)
            sp.dma_start(w0_swap_sb, w0_swap).then_inc(weights_in, 16)
            sp.dma_start(wd_sb[:, :], w0_diag).then_inc(weights_in, 16)
            for n, w in enumerate((w1, w2)):
                sp.dma_start(w12_sb[n][:, :, :], w.rearrange("(t a) h k -> (a h) t k", a=2))\
                    .then_inc(weights_in, 16)
            sp.dma_start(b1_sb[:, :], b_top1.rearrange("(t p) -> p t", p=P),
                         allow_slow_non_contiguous=True).then_inc(weights_in, 16)
            sp.dma_start(b2_sb[:, :], b_top2.rearrange("(t p) -> p t", p=P),
                         allow_slow_non_contiguous=True).then_inc(weights_in, 16)
            sp.wait_ge(x0_ready, 1)
            load_shifted(0)
            load_group(0, 0, rep0_in[0])
            for g in (1, 2, 3):
                load_group(0, g, rep_in[g])
            sp.wait_ge(gathered[0], gathered_count(0, 0))
            load_ids(2, 0)
            sp.wait_ge(x0_ready, 2)
            sp.wait_ge(shifted_in, 16 * NSHIFT)
            sp.wait_ge(slot_full, slot_of(0, 0, 0) + L0_SLOTS)
            load_shifted(1)
            load_group(1, 0, rep0_in[1])

            def tile(i, q):
                if exists(i + 3):
                    sp.wait_ge(gathered[1 - q], gathered_count(i + 1, 1 - q))
                    load_ids(i + 3, 1 - q)
                for p in range(2):
                    after = following(i, p)

                    def next_but_one_shifted():
                        sp.wait_ge(x0_ready, 2 * i + p + 3)
                        sp.wait_ge(slot_full, slot_of(*after, 0) + L0_SLOTS)
                        load_shifted(p)

                    early = not is_int(2 * i + p, 0)
                    if exists(i + 1) and early:
                        next_but_one_shifted()
                    if exists(after[0]):
                        load_groups123(*after, (i, p))
                    if exists(i + 1) and not early:
                        next_but_one_shifted()
                    if exists(i + 1):
                        sp.wait_ge(pool_full, pool_run(i, p, 2) + 1)
                        load_group(p, 0, rep0_in[p])

            all_turns(sp, tile)

            for half in range(2):
                sp.dma_start(wt1_z[H * half:H * half + H, :, :],
                             w_top1[0:ZD, :].rearrange("(l k) n -> k l n", k=H)).then_inc(mlp_in, 16)
            sp.dma_start(wt1_d, w_top1[ZD:ZD + D, :]).then_inc(mlp_in, 16)
            sp.dma_start(wt2, w_top2.rearrange("(t p) n -> p t n", p=P)).then_inc(mlp_in, 16)
            sp.dma_start(wt3, w_top3.rearrange("(t p) o -> p (t o)", p=P),
                         allow_slow_non_contiguous=True).then_inc(mlp_in, 16)
            for g in (1, 2, 3):
                sp.wait_ge(rep_in[g], 16 * GROUP_DMAS * STEPS)
            for n in range(2):
                sp.wait_ge(rep0_in[n], 16 * GROUP_DMAS * TILES)
                sp.dma_start(dense_sb[n], dense_t[:, COLS * n:COLS * (n + 1)]).then_inc(mlp_in, 16)
            sp.wait_ge(mlp_out, (B // CH) * (F1 // P + F2 // P + 1))
            sp.dma_start(out.rearrange("b o -> o b"), y_sb).then_inc(y_stored, 16)
            sp.wait_ge(y_stored, 16)

        @block.gpsimd
        def _(pool):
            def gather(q, ms):
                for m in ms:
                    nc.gpsimd.indirect_dma_start(
                        emb[q][:, m, :], None, tables[m][:, :],
                        bass.IndirectOffsetOnAxis(ap=ids_sb[q][:, m:m + 1], axis=0),
                    ).then_inc(gathered[q], 16)

            pool.wait_ge(ids_in, 32)
            gather(0, range(M))
            nc.gpsimd.memset(ident[:, :], 0.0).then_inc(ident_made, 1)
            pool.wait_ge(ident_made, 1)
            nc.gpsimd.affine_select(out=ident[:, :], in_=ident[:, :], compare_op=ALU.not_equal, fill=1.0,
                                    base=0, pattern=[[-1, P]], channel_multiplier=1).then_inc(ident_made, 1)
            gather(1, range(M // 2))
            pool.wait_ge(w0_summed, 1)

            def products(i, p, layer):
                run = pool_run(i, p, layer)
                if layer == 1:
                    pool.wait_ge(rep0_in[p], (i + 1) * 16 * GROUP_DMAS)
                pool.wait_ge(x_pool_ready, run + 1)
                if not is_int(run, 0):
                    pool.wait_ge(pool_used, run)
                nc.gpsimd.tensor_tensor(
                    pool_prod[:, :, :, :],
                    x_pool[p][:, :, :].unsqueeze(2).broadcast_to([P, 2, POOL_MT, CH]),
                    rep_tiles(p, 0, POOL_MT).rearrange("p t (c n) -> p c t n", c=2),
                    ALU.mult).then_inc(pool_full, 1)

            def tile(i, q):
                if exists(i + 2):
                    pool.wait_ge(ids_in, 16 * (i + 3))
                    pool.wait_ge(transposed, 2 * i + 2)
                quarter = M // 4
                for p in range(2):
                    for layer in (1, 2):
                        products(i, p, layer)
                        if is_int(2 * i + p, 0):
                            if layer == 1:
                                gather(1, range(M // 2, M))
                        elif is_int(i, 0):
                            gather(q, range(M // 2 * (layer - 1), M // 2 * layer))
                        elif exists(i + 2):
                            first = quarter * (2 * p + layer - 1)
                            gather(q, range(first, first + quarter))

            all_turns(pool, tile)

        @block.vector
        def _(dve):
            def product(i, p, layer, k, x, x0):
                n = slot_of(i, p, layer, k)
                if not is_int(n, *range(NSLOT)):
                    dve.wait_ge(slot_used, n - NSLOT + 1)
                nc.vector.tensor_tensor(slots[slot_buffer(i, p, layer, k)][:, :, :, :],
                                        x.unsqueeze(2).broadcast_to([P, 2, SLOT_MT, CH]),
                                        x0.rearrange("p t (c n) -> p c t n", c=2),
                                        ALU.mult).then_inc(slot_full, 1)

            def layer0(i, p):
                s = 2 * i + p
                dve.wait_ge(x0_ready, s + 1)
                dve.wait_ge(shifted_in, 16 * NSHIFT * (s + 1))
                for k in range(L0_SLOTS):
                    product(i, p, 0, k, x0t[p][:, :].rearrange("p (c n) -> p c n", c=2),
                            shifted[:, SLOT_MT * k:SLOT_MT * (k + 1), :])

            def layer12(i, p, layer, ks):
                for k in ks:
                    t = POOL_MT + SLOT_MT * k
                    if k == 0:
                        dve.wait_ge(x_ready, 2 * (2 * i + p) + layer)
                        if layer == 1:
                            dve.wait_ge(rep0_in[p], (i + 1) * 16 * GROUP_DMAS)
                    if layer == 1 and t % GROUP == 0:
                        dve.wait_ge(rep_in[t // GROUP], (2 * i + p + 1) * 16 * GROUP_DMAS)
                    product(i, p, layer, k, x_ps[p][:, :, :], rep_tiles(p, t, SLOT_MT))

            def sum_over_d(i, p, layer):
                run = run_of(i, p, layer)
                dve.wait_ge(acc_used, run + 1)
                nc.vector.tensor_reduce(zhalf[p][:, layer, :],
                                        stacked[run_parity(i, p, layer)][:, :].rearrange("p (d b) -> p b d", d=DC),
                                        AX.X, ALU.add).then_inc(summed, 1)
                if p == 1:
                    dve.wait_ge(summed, run + 1)
                    nc.vector.tensor_tensor(z[:, layer, bass.ts(i, P)], zhalf[0][:, layer, :],
                                            zhalf[1][:, layer, :], ALU.add).then_inc(z_ready, 1)

            dve.wait_ge(weights_in, 16 * 7)
            nc.vector.tensor_tensor(w0_sb[:, 0:L0_MT - 1, :], w0_sb[:, 0:L0_MT - 1, :],
                                    w0_swap_sb[:, 0:L0_MT - 1, :], ALU.add)
            nc.vector.tensor_tensor(w0_sb[0:P - M, L0_MT - 1, :], w0_sb[0:P - M, L0_MT - 1, :],
                                    w0_swap_sb[0:P - M, L0_MT - 1, :], ALU.add).then_inc(w0_summed, 1)
            layer0(0, 0)
            sum_over_d(0, 0, 0)

            def tile(i, q):
                for p in range(2):
                    after = following(i, p)
                    layer12(i, p, 1, range(0, 3))
                    if not is_int(2 * i + p, 0):
                        sum_over_d(*((i - 1, 1) if p == 0 else (i, 0)), 2)
                    layer12(i, p, 1, range(3, L12_SLOTS))
                    if exists(after[0]):
                        layer0(*after)
                    layer12(i, p, 2, range(0, 2))
                    sum_over_d(i, p, 1)
                    layer12(i, p, 2, range(2, 4))
                    if exists(after[0]):
                        sum_over_d(*after, 0)
                    layer12(i, p, 2, range(4, L12_SLOTS))

            all_turns(dve, tile)
            sum_over_d(TILES - 1, 1, 2)

        @block.tensor
        def _(pe):
            def transpose(i, q, p):
                s = 2 * i + p
                if p == 0:
                    pe.wait_ge(gathered[q], gathered_count(i, q))
                if not is_int(s, 0):
                    pe.wait_ge(x0_ready, s)
                for c in range(2):
                    for d in range(DC):
                        last = nc.tensor.transpose(tr[0:M, c, P * d:P * (d + 1)],
                                                   emb[q][:, :, (2 * p + c) * DC + d], ident[:, :])
                last.then_inc(transposed, 1)

            def pair_tile(bank, weight, moving, start, stop):
                for c in range(2):
                    last = nc.tensor.matmul(bank[H * c:H * c + H, :], weight, moving[:, c, :],
                                            start=start, stop=stop)
                return last

            def take_bank(i, p, layer):
                run = run_of(i, p, layer)
                if not is_int(run, 0, 1):
                    pe.wait_ge(acc_used, run - 1)
                return acc[run_parity(i, p, layer)]

            def from_slots(i, p, layer, bank, weights, first, ks):
                for k in ks:
                    pe.wait_ge(slot_full, slot_of(i, p, layer, k) + 1)
                    for j in range(SLOT_MT):
                        last = pair_tile(bank, weights[:, first + SLOT_MT * k + j, :],
                                         slots[slot_buffer(i, p, layer, k)][:, :, j, :],
                                         start=layer > 0 and (k, j) == (0, 0),
                                         stop=layer == 0 and (k, j) == (L0_SLOTS - 1, SLOT_MT - 1))
                    last.then_inc(slot_used, 1)

            def layer0(i, p):
                bank = take_bank(i, p, 0)
                pe.wait_ge(x0_ready, 2 * i + p + 1)
                pair_tile(bank, wd_sb[:, :], squares[p][:, :].rearrange("p (c n) -> p c n", c=2), True, False)
                from_slots(i, p, 0, bank, w0_sb, 0, range(L0_SLOTS))

            def layer12(i, p, layer, between=None):
                bank = take_bank(i, p, layer)
                weights = w12_sb[layer - 1]
                from_slots(i, p, layer, bank, weights, POOL_MT, range(TR_SLOT))
                if between:
                    transpose(*between)
                from_slots(i, p, layer, bank, weights, POOL_MT, range(TR_SLOT, L12_SLOTS))
                pe.wait_ge(pool_full, pool_run(i, p, layer) + 1)
                for t in range(POOL_MT):
                    last = pair_tile(bank, weights[:, t, :], pool_prod[:, :, t, :], False, t == POOL_MT - 1)
                last.then_inc(pool_used, 1)

            pe.wait_ge(weights_in, 16 * 7)
            pe.wait_ge(ident_made, 2)
            pe.wait_ge(w0_summed, 1)
            transpose(0, 0, 0)
            layer0(0, 0)
            transpose(0, 0, 1)

            def tile(i, q):
                for p in range(2):
                    after = following(i, p)
                    next_but_one = (i + 1, 1 - q, p) if exists(i + 1) else None
                    early = not is_int(2 * i + p, 0)
                    layer12(i, p, 1, between=next_but_one if early else None)
                    if exists(after[0]):
                        layer0(*after)
                    layer12(i, p, 2)
                    if not early:
                        transpose(*next_but_one)

            all_turns(pe, tile)

            pe.wait_ge(mlp_in, 16 * 7)
            pe.wait_ge(z_ready, NLAYER * TILES)
            pe.wait_ge(acc_used, NLAYER * STEPS)
            u = 0
            for n in range(B // CH):
                cols = slice(CH * n, CH * (n + 1))
                dense = dense_sb[n // 2][:, CH * (n % 2):CH * (n % 2 + 1)]
                for t in range(F1 // P):
                    if u >= 4:
                        pe.wait_ge(mlp_out, u - 3)
                    for l in range(NLAYER):
                        nc.tensor.matmul(mlp_banks[u % 4], wt1_z[:, l, P * t:P * (t + 1)], z[:, l, cols],
                                         start=(l == 0), stop=False)
                    nc.tensor.matmul(mlp_banks[u % 4], wt1_d[:, P * t:P * (t + 1)], dense,
                                     start=False, stop=True).then_inc(mlp_full, 1)
                    u += 1
            for n in range(B // CH):
                cols = slice(CH * n, CH * (n + 1))
                for t in range(F2 // P):
                    pe.wait_ge(mlp_out, max(u - 3, (n + 1) * (F1 // P)))
                    for q in range(F1 // P):
                        last = nc.tensor.matmul(mlp_banks[u % 4], wt2[:, q, P * t:P * (t + 1)], h1[:, q, cols],
                                                start=(q == 0), stop=(q == F1 // P - 1))
                    last.then_inc(mlp_full, 1)
                    u += 1
            for n in range(B // CH):
                cols = slice(CH * n, CH * (n + 1))
                pe.wait_ge(mlp_out, max(u - 3, (B // CH) * (F1 // P) + (n + 1) * (F2 // P)))
                for q in range(F2 // P):
                    last = nc.tensor.matmul(mlp_banks[u % 4][0:1, :], wt3[:, q:q + 1], h2[:, q, cols],
                                            start=(q == 0), stop=(q == F2 // P - 1))
                last.then_inc(mlp_full, 1)
                u += 1

        @block.scalar
        def _(act):
            def take_x0(i, p):
                s = 2 * i + p
                act.wait_ge(transposed, s + 1)
                if not is_int(i, 0):
                    act.wait_ge(rep0_in[p], i * 16 * GROUP_DMAS)
                    for g in (1, 2, 3):
                        act.wait_ge(rep_in[g], (s - 1) * 16 * GROUP_DMAS)
                for g in range(P // M):
                    nc.scalar.activation(x0t[p][M * g:M * g + M, :].rearrange("p (c n) -> p c n", c=2),
                                         tr[0:M, :, :], ACT.Copy)
                nc.scalar.activation(squares[p][:, :].rearrange("p (c n) -> p c n", c=2), tr[0:M, :, :],
                                     ACT.Square).then_inc(x0_ready, 1)

            def finish(i, p, layer):
                run = run_of(i, p, layer)
                bank = acc[run_parity(i, p, layer)]
                if layer == 0:
                    act.wait_ge(slot_used, slot_of(i, p, 0) + L0_SLOTS)
                else:
                    act.wait_ge(pool_used, pool_run(i, p, layer) + 1)
                def both_halves(x):
                    for c in range(2):
                        for half in range(2):
                            last = nc.scalar.activation(x[H * half:H * half + H, c, :],
                                                        bank[H * c:H * c + H, :], ACT.Relu)
                    return last

                if layer < 2:
                    both_halves(x_ps[p]).then_inc(x_ready, 1)
                    if layer == 1:
                        act.wait_ge(pool_full, pool_run(i, p, 1) + 1)
                    elif not is_int(i, 0):
                        act.wait_ge(pool_full, pool_run(i - 1, p, 2) + 1)
                    both_halves(x_pool[p]).then_inc(x_pool_ready, 1)
                if not is_int(run, 0, 1):
                    act.wait_ge(summed, run - 1)
                nc.scalar.activation(stacked[run_parity(i, p, layer)][:, :], bank[:, :], ACT.Relu)\
                    .then_inc(acc_used, 1)

            take_x0(0, 0)
            finish(0, 0, 0)
            take_x0(0, 1)

            def tile(i, q):
                for p in range(2):
                    after = following(i, p)
                    early = not is_int(2 * i + p, 0)
                    if exists(i + 1) and early:
                        take_x0(i + 1, p)
                    finish(i, p, 1)
                    if exists(after[0]):
                        finish(*after, 0)
                    finish(i, p, 2)
                    if not early:
                        take_x0(i + 1, p)

            all_turns(act, tile)

            act.wait_ge(weights_in, 16 * 7)
            act.wait_ge(slot_full, slot_of(TILES - 1, 1, 2) + L12_SLOTS)
            act.wait_ge(pool_full, pool_run(TILES - 1, 1, 2) + 1)
            u = 0
            for bias, hidden, width in ((b1_sb, h1, F1), (b2_sb, h2, F2)):
                for n in range(B // CH):
                    for t in range(width // P):
                        act.wait_ge(mlp_full, u + 1)
                        nc.scalar.activation(hidden[:, t, CH * n:CH * (n + 1)], mlp_banks[u % 4], ACT.Relu,
                                             bias=bias[:, t:t + 1]).then_inc(mlp_out, 1)
                        u += 1
            for n in range(B // CH):
                act.wait_ge(mlp_full, u + 1)
                nc.scalar.activation(y_sb[:, CH * n:CH * (n + 1)], mlp_banks[u % 4][0:1, :], ACT.Copy)\
                    .then_inc(mlp_out, 1)
                u += 1


def kernel(**inputs):
    import numpy as np
    import concourse.bacc as bacc
    from concourse import mybir as mb
    from concourse.bass_utils import run_bass_kernel_spmd

    w0 = np.asarray(inputs["L0_rec_W0"])
    m = np.arange(M)[None, :, None]
    shift = (np.arange(P // M)[:, None, None] + 1) + P // M * np.arange(L0_MT)[None, None, :]
    h = (m + shift) % M
    m = np.broadcast_to(m, h.shape)
    named = {
        "dense_t": np.ascontiguousarray(np.asarray(inputs["dense_ctx"]).T),
        "ids": np.ascontiguousarray(inputs["ids"]),
        **{f"tbl_{n}": np.ascontiguousarray(inputs[f"tbl_{n}"]) for n in range(M)},
        **{k: np.ascontiguousarray(inputs[k]) for k in ("W_top1", "b_top1", "W_top2", "b_top2", "W_top3")},
        "w0_pair": np.ascontiguousarray(w0[m, h].reshape(P, L0_MT, H)),
        "w0_swap": np.ascontiguousarray(w0[h, m].reshape(P, L0_MT, H)),
        "w0_diag": np.ascontiguousarray(w0[np.arange(M), np.arange(M)]),
        "W1": np.ascontiguousarray(inputs["L0_rec_W1"]),
        "W2": np.ascontiguousarray(inputs["L0_rec_W2"]),
    }
    nc = bacc.Bacc("TRN2", target_bir_lowering=False, num_devices=1)
    args = {k: nc.dram_tensor(f"in_{k}", a.shape, mb.dt.from_np(a.dtype), kind="ExternalInput").ap()
            for k, a in named.items()}
    out = nc.dram_tensor("out_y", (B, 1), mb.dt.float32, kind="ExternalOutput").ap()
    cin(nc, args["dense_t"], args["ids"], [args[f"tbl_{n}"] for n in range(M)], args["W_top1"],
        args["b_top1"], args["W_top2"], args["b_top2"], args["W_top3"], args["w0_pair"], args["w0_swap"],
        args["w0_diag"], args["W1"], args["W2"], out)
    r = run_bass_kernel_spmd(nc, [{f"in_{k}": a for k, a in named.items()}], core_ids=[0])
    return r.results[0]["out_y"]
```

```python
import concourse.bass as bass
from concourse import mybir
from contextlib import ExitStack

F32 = mybir.dt.float32
I32 = mybir.dt.int32
ALU = mybir.AluOpType
ACT = mybir.ActivationFunctionType
AX = mybir.AxisListType

P = 128
B, M, D, H = 2048, 32, 16, 64
NLAYER = 3
TILES = B // P
STEPS = 2 * TILES
CH = 512
DC = CH // P
COLS = 2 * CH
MT = M // 2
POOL_MT = {1: 3, 2: 4}
NSHIFT = M // 2
L0_MT = NSHIFT * M // P
GROUP = 4
SLOT_MT = 2
NSLOT = 4
L0_SLOTS = L0_MT // SLOT_MT
SLOT_WIDTHS = {1: (1, 2, 2, 2, 2, 2, 2), 2: (1, 2, 2, 2, 2, 2, 1)}
L12_SLOTS = len(SLOT_WIDTHS[1])
STEP_SLOTS = 2 * L12_SLOTS + L0_SLOTS
TURNS = range(1, TILES // 2 - 2)
FIRST_GATHERS = 28
TR_SLOT = 4
SUM_SLOT = 5
POOL_SLOT = {1: 2, 2: 5}
GROUP_DMAS = GROUP * 2
F1, F2 = 512, 256
EARLY = TILES - CH // P


def following(i, p):
    return (i, 1) if p == 0 else (i + 1, 0)


def is_int(x, *values):
    return isinstance(x, int) and x in values


def slot_of(i, p, layer, k=0):
    s = 2 * i + p
    if layer == 0:
        return k if is_int(s, 0) else L0_SLOTS + (s - 1) * STEP_SLOTS + L12_SLOTS + k
    if layer == 1:
        return L0_SLOTS + s * STEP_SLOTS + k
    between = 0 if is_int(s, STEPS - 1) else L0_SLOTS
    return L0_SLOTS + s * STEP_SLOTS + L12_SLOTS + between + k


def slot_tiles(layer, k):
    return POOL_MT[layer] + sum(SLOT_WIDTHS[layer][:k]), SLOT_WIDTHS[layer][k]


def run_of(i, p, layer):
    s = 2 * i + p
    if layer == 0:
        return 0 if is_int(s, 0) else 3 * s - 1
    return 3 * s + 1 if layer == 1 else (3 * s + 2 if is_int(s, STEPS - 1) else 3 * s + 3)


def exists(i):
    return not isinstance(i, int) or i < TILES


def gathered_count(i, q):
    return 16 * M // 2 * (i - q + 2)


def all_turns(engine, tile):
    for i in range(2 * TURNS.start):
        tile(i, i % 2)
    with engine.Fori(TURNS.start, TURNS.stop) as j:
        for q in range(2):
            tile(2 * j + q, q)
    for i in range(2 * TURNS.stop, TILES):
        tile(i, i % 2)


def some_tile(i):
    return i if isinstance(i, int) else 1


def slot_buffer(i, p, layer, k):
    return slot_of(some_tile(i), p, layer, k) % NSLOT


def run_parity(i, p, layer):
    return run_of(some_tile(i), p, layer) % 2


def pool_run(i, p, layer):
    return 2 * (2 * i + p) + layer - 1


def cin(nc, dense_t, ids, tables, w_top1, b_top1, w_top2, b_top2, w_top3, w0_pair, w0_swap, w0_diag,
        w1, w2, z_dram, out):
    ctx = ExitStack()
    with ctx:
        def sb(name, shape, dt=F32):
            return ctx.enter_context(nc.sbuf_tensor(name, shape, dt))

        def sem(name):
            return ctx.enter_context(nc.semaphore(name))

        ident = sb("ident", [P, P])
        ids_sb = [sb(f"ids_sb{q}", [P, M], I32) for q in range(2)]
        emb = [sb(f"emb{q}", [P, M, D]) for q in range(2)]
        x0t = [sb(f"x0t{p}", [P, COLS]) for p in range(2)]
        squares = sb("squares", [2 * M, COLS])
        shifted = sb("shifted", [P, L0_MT, COLS])
        rep0 = [sb(f"rep0_{p}", [P, GROUP, COLS]) for p in range(2)]
        rep123 = sb("rep123", [P, MT - GROUP, COLS])
        slots = [sb(f"slot{n}", [P, 2, SLOT_MT, CH]) for n in range(NSLOT)]
        pool_prod = {layer: sb(f"pool_prod{layer}", [P, 2, n, CH]) for layer, n in POOL_MT.items()}
        x_pool = [sb(f"x_pool{p}", [P, 2, CH]) for p in range(2)]
        stacked = [sb(f"stacked{p}", [P, CH]) for p in range(2)]
        zhalf = [sb(f"zhalf{p}", [P, NLAYER, P]) for p in range(2)]
        zother = sb("zother", [P, NLAYER, P])
        z_tile = sb("z_tile", [P, 2, P])
        z_last = sb("z_last", [P, 2, CH])
        w0_sb = sb("w0_sb", [P, L0_MT, H])
        wd_sb = sb("wd_sb", [2 * M, H])
        w12_sb = [sb(f"w{n}_sb", [P, MT, H]) for n in (1, 2)]
        b1_sb = sb("b1_sb", [P, F1 // P])
        b2_sb = sb("b2_sb", [P, F2 // P])
        w0_swap_sb = pool_prod[1][:, 0, 0, 0:L0_MT * H].rearrange("p (j k) -> p j k", j=L0_MT)

        sh = shifted[:, :, :].rearrange("p a b -> p (a b)")
        wt1 = [sh[:, F1 * n:F1 * (n + 1)] for n in range(2)]
        wt2 = sh[:, 4 * F1:4 * F1 + 4 * F2].rearrange("p (t n) -> p t n", t=F1 // P)
        wt3 = sh[:, 4 * F1 + 4 * F2:4 * F1 + 4 * F2 + F2 // P]
        h1 = rep123[:, 0:8, :].rearrange("p a b -> p (a b)").rearrange("p (t n) -> p t n", t=F1 // P)
        z_early = rep0[0][:, 0:3, :].rearrange("p a b -> p (a b)").rearrange("p (l n) -> p l n", l=2)
        h2 = rep123[:, 8:12, :].rearrange("p a b -> p (a b)").rearrange("p (t n) -> p t n", t=F2 // P)
        y_sb = rep0[1][:, 0, 0:CH]

        acc = [ctx.enter_context(nc.psum_tensor(f"acc{n}", [P, CH], F32)) for n in range(2)]
        x_ps = [ctx.enter_context(nc.psum_tensor(f"x_ps{n}", [P, 2, CH], F32)) for n in range(2)]
        tr = ctx.enter_context(nc.psum_tensor("tr", [P, 2, CH], F32))

        weights_in = sem("weights_in")
        w0_summed = sem("w0_summed")
        ident_made = sem("ident_made")
        ids_in = sem("ids_in")
        gathered = [sem(f"gathered{q}") for q in range(2)]
        transposed = sem("transposed")
        x0_halfway = sem("x0_halfway")
        x0_ready = sem("x0_ready")
        shifted_in = [sem(f"shifted_in{k}") for k in range(L0_SLOTS)]
        rep0_in = [sem(f"rep0_in{p}") for p in range(2)]
        rep_in = [None] + [sem(f"rep{g}_in") for g in (1, 2, 3)]
        slot_full = sem("slot_full")
        slot_used = sem("slot_used")
        pool_full = sem("pool_full")
        pool_used = sem("pool_used")
        acc_used = sem("acc_used")
        x_ready = sem("x_ready")
        x_pool_ready = sem("x_pool_ready")
        summed = sem("summed")
        z_summed = sem("z_summed")
        z_moved = sem("z_moved")
        z_ready = sem("z_ready")
        z_stored = sem("z_stored")
        mlp_in = sem("mlp_in")
        mlp_full = sem("mlp_full")
        mlp_out = sem("mlp_out")
        y_stored = sem("y_stored")

        mlp_banks = [tr[:, 0, :], tr[:, 1, :], acc[0][:, :], acc[1][:, :]]
        block = ctx.enter_context(nc.Block())

        def rep_tiles(p, t0, n):
            if t0 < GROUP:
                return rep0[p][:, t0:t0 + n, :]
            return rep123[:, t0 - GROUP:t0 - GROUP + n, :]

        @block.sync
        def _(sp):
            def load_ids(i, q):
                sp.dma_start(ids_sb[q][:, :], ids[bass.ts(i, P), :]).then_inc(ids_in, 16)

            def load_shifted(p, k, odds=(0, 1)):
                for j in range(SLOT_MT * k, SLOT_MT * (k + 1)):
                    for g in range(P // M):
                        if g % 2 not in odds:
                            continue
                        q = P // M * j + g + 1 + (P // 2 if g % 2 else 0)
                        sp.dma_start(shifted[M * g:M * g + M, j, :], x0t[p][q:q + M, :])\
                            .then_inc(shifted_in[k], 16)

            def load_group(p, g, signal):
                for m in range(2 * GROUP * g, 2 * GROUP * (g + 1)):
                    lo = H * (m % 2)
                    src = x0t[p][lo + m % M:lo + m % M + 1, :]
                    sp.dma_start(rep_tiles(p, m // 2, 1)[lo:lo + H, 0, :],
                                 src.unsqueeze(1).broadcast_to([1, H, COLS])).then_inc(signal, 16)

            def load_groups123(i, p, before):
                for g in (1, 2, 3):
                    sp.wait_ge(slot_full, slot_of(*before, 2, 2 * g) + 1)
                    load_group(p, g, rep_in[g])

            load_ids(0, 0)
            load_ids(1, 1)
            sp.dma_start(w0_sb[:, :, :], w0_pair).then_inc(weights_in, 16)
            sp.dma_start(w0_swap_sb, w0_swap).then_inc(weights_in, 16)
            for p in range(2):
                sp.dma_start(wd_sb[M * p:M * p + M, :], w0_diag).then_inc(weights_in, 16)
            for n, w in enumerate((w1, w2)):
                sp.dma_start(w12_sb[n][:, :, :], w.rearrange("(t a) h k -> (a h) t k", a=2))\
                    .then_inc(weights_in, 16)
            sp.dma_start(b1_sb[:, :], b_top1.rearrange("(t p) -> p t", p=P),
                         allow_slow_non_contiguous=True).then_inc(weights_in, 16)
            sp.dma_start(b2_sb[:, :], b_top2.rearrange("(t p) -> p t", p=P),
                         allow_slow_non_contiguous=True).then_inc(weights_in, 16)
            sp.dma_start(z_last[H:H + D, 1, :], dense_t[:, P * EARLY:]).then_inc(mlp_in, 16)
            sp.wait_ge(gathered[0], gathered_count(0, 0))
            load_ids(2, 0)
            sp.wait_ge(x0_halfway, 1)
            load_shifted(0, 0, odds=[0])
            sp.wait_ge(x0_ready, 1)
            load_shifted(0, 0, odds=[1])
            load_shifted(0, 1)
            load_group(0, 0, rep0_in[0])
            for g in (1, 2, 3):
                load_group(0, g, rep_in[g])
            sp.wait_ge(x0_ready, 2)
            for k in range(L0_SLOTS):
                sp.wait_ge(slot_full, slot_of(0, 0, 0, k) + 1)
                load_shifted(1, k)
            load_group(1, 0, rep0_in[1])

            def store_z(i):
                sp.wait_ge(z_ready, i + 1)
                sp.dma_start(z_dram[0, :, bass.ts(i, P)], z_tile[:, 0, :]).then_inc(z_stored, 16)
                sp.dma_start(z_dram[1, 0:H, bass.ts(i, P)], z_tile[0:H, 1, :]).then_inc(z_stored, 16)

            def tile(i, q):
                for p in range(2):
                    after = following(i, p)
                    if p == 1 and exists(i + 3):
                        sp.wait_ge(gathered[1 - q], gathered_count(i + 1, 1 - q))
                        load_ids(i + 3, 1 - q)
                    if exists(i + 1):
                        sp.wait_ge(slot_full, slot_of(i, p, 2, 0) + 1)
                        load_shifted(p, 0)
                    if exists(after[0]):
                        load_groups123(*after, (i, p))
                    if exists(i + 1):
                        load_shifted(p, 1)
                        sp.wait_ge(pool_full, pool_run(i, p, 2) + 1)
                        load_group(p, 0, rep0_in[p])
                if not is_int(i, 0, *range(EARLY + 1, TILES)):
                    store_z(i - 1)

            all_turns(sp, tile)

            sp.wait_ge(pool_full, pool_run(TILES - 1, 0, 2) + 1)
            sp.wait_ge(z_stored, 32 * EARLY)
            sp.dma_start(z_early[:, 0, :], z_dram[0, :, 0:P * EARLY]).then_inc(mlp_in, 16)
            sp.dma_start(z_early[0:H, 1, :], z_dram[1, 0:H, 0:P * EARLY]).then_inc(mlp_in, 16)
            sp.dma_start(z_early[H:H + D, 1, :], dense_t[:, 0:P * EARLY]).then_inc(mlp_in, 16)
            sp.dma_start(wt1[0], w_top1[0:2 * H, :]).then_inc(mlp_in, 16)
            sp.dma_start(wt1[1][0:H + D, :], w_top1[2 * H:, :]).then_inc(mlp_in, 16)
            sp.dma_start(wt2, w_top2.rearrange("(t p) n -> p t n", p=P)).then_inc(mlp_in, 16)
            sp.dma_start(wt3, w_top3.rearrange("(t p) o -> p (t o)", p=P),
                         allow_slow_non_contiguous=True).then_inc(mlp_in, 16)
            sp.wait_ge(mlp_out, (B // CH) * (F1 // P + F2 // P) + 1)
            sp.dma_start(out.rearrange("(n c) o -> n (c o)", c=CH), y_sb[0:P:P // (B // CH), :])\
                .then_inc(y_stored, 16)
            sp.wait_ge(y_stored, 16)

        @block.gpsimd
        def _(pool):
            def gather(q, ms):
                for m in ms:
                    nc.gpsimd.indirect_dma_start(
                        emb[q][:, m, :], None, tables[m][:, :],
                        bass.IndirectOffsetOnAxis(ap=ids_sb[q][:, m:m + 1], axis=0),
                    ).then_inc(gathered[q], 16)

            nc.gpsimd.memset(ident[:, :], 0.0).then_inc(ident_made, 1)
            pool.wait_ge(ident_made, 1)
            nc.gpsimd.affine_select(out=ident[:, :], in_=ident[:, :], compare_op=ALU.not_equal, fill=1.0,
                                    base=0, pattern=[[-1, P]], channel_multiplier=1).then_inc(ident_made, 1)
            pool.wait_ge(ids_in, 32)
            gather(0, range(M))
            gather(1, range(FIRST_GATHERS))
            pool.wait_ge(w0_summed, 1)

            def products(i, p, layer):
                run = pool_run(i, p, layer)
                if layer == 1:
                    pool.wait_ge(rep0_in[p], (i + 1) * 16 * GROUP_DMAS)
                pool.wait_ge(x_pool_ready, run + 1)
                if not is_int(run, 0, 1):
                    pool.wait_ge(pool_used, run - 1)
                nc.gpsimd.tensor_tensor(
                    pool_prod[layer][:, :, :, :],
                    x_pool[p][:, :, :].unsqueeze(2).broadcast_to([P, 2, POOL_MT[layer], CH]),
                    rep_tiles(p, 0, POOL_MT[layer]).rearrange("p t (c n) -> p c t n", c=2),
                    ALU.mult).then_inc(pool_full, 1)

            def await_next(i):
                pool.wait_ge(ids_in, 16 * (i + 3))
                pool.wait_ge(transposed, 2 * i + 2)

            def tile(i, q):
                for p in range(2):
                    if p == 0 and exists(i + 2) and not is_int(i, 0):
                        await_next(i)
                    products(i, p, 1)
                    middle = M // 2
                    if is_int(i, 0):
                        middle = M // 2 - (M - FIRST_GATHERS)
                        if p == 0:
                            gather(1, range(FIRST_GATHERS, M))
                            await_next(0)
                    if exists(i + 2):
                        gather(q, range(middle, M) if p else range(middle))
                    products(i, p, 2)

            all_turns(pool, tile)

        @block.vector
        def _(dve):
            def product(i, p, layer, k, x, x0):
                n = slot_of(i, p, layer, k)
                if not is_int(n, *range(NSLOT)):
                    dve.wait_ge(slot_used, n - NSLOT + 1)
                width = x0.shape[1]
                chunks = slice(0, 2)
                if layer == 2 and k == 0:
                    taken = 2 * (2 * (2 * i + p) + layer - 1)
                    dve.wait_ge(x_ready, taken + 1)
                    nc.vector.tensor_tensor(slots[slot_buffer(i, p, layer, k)][:, 0, 0:width, :],
                                            x[:, 0, :].unsqueeze(1).broadcast_to([P, width, CH]),
                                            x0[:, :, 0:CH], ALU.mult)
                    dve.wait_ge(x_ready, taken + 2)
                    chunks = slice(1, 2)
                nc.vector.tensor_tensor(slots[slot_buffer(i, p, layer, k)][:, chunks, 0:width, :],
                                        x[:, chunks, :].unsqueeze(2).broadcast_to(
                                            [P, chunks.stop - chunks.start, width, CH]),
                                        x0.rearrange("p t (c n) -> p c t n", c=2)[:, chunks],
                                        ALU.mult).then_inc(slot_full, 1)

            def layer0(i, p):
                s = 2 * i + p
                dve.wait_ge(x0_ready, s + 1)
                for k in range(L0_SLOTS):
                    dve.wait_ge(shifted_in[k], 16 * NSHIFT // L0_SLOTS * (s + 1))
                    product(i, p, 0, k, x0t[p][:, :].rearrange("p (c n) -> p c n", c=2),
                            shifted[:, SLOT_MT * k:SLOT_MT * (k + 1), :])

            def layer12(i, p, layer, ks):
                for k in ks:
                    t, width = slot_tiles(layer, k)
                    if layer == 1:
                        if k == 0:
                            dve.wait_ge(rep0_in[p], (i + 1) * 16 * GROUP_DMAS)
                            dve.wait_ge(x_ready, 4 * (2 * i + p) + 2)
                        for g in (1, 2, 3):
                            if GROUP * g in range(t, t + width):
                                dve.wait_ge(rep_in[g], (2 * i + p + 1) * 16 * GROUP_DMAS)
                    product(i, p, layer, k, x_ps[p][:, :, :], rep_tiles(p, t, width))

            def sum_over_d(i, p, layer):
                run = run_of(i, p, layer)
                if p == 1 and layer == 0 and not is_int(i, 0):
                    dve.wait_ge(z_ready, i)
                dve.wait_ge(acc_used, run + 1)
                nc.vector.tensor_reduce(zhalf[p][:, layer, :],
                                        stacked[run_parity(i, p, layer)][:, :].rearrange("p (d b) -> p b d", d=DC),
                                        AX.X, ALU.add).then_inc(summed, 1)
                if p == 1:
                    dve.wait_ge(summed, run + 1)
                    total = nc.vector.tensor_tensor(zhalf[1][:, layer, :], zhalf[0][:, layer, :],
                                                    zhalf[1][:, layer, :], ALU.add)
                    if layer == 2:
                        total.then_inc(z_summed, 1)

            def add_chunks(i):
                dve.wait_ge(z_moved, i + 1)
                if is_int(i, *range(EARLY, TILES)):
                    z, cols = z_last, bass.ts(i - EARLY, P)
                else:
                    z, cols = z_tile, slice(0, P)
                    if not is_int(i, 0):
                        dve.wait_ge(z_stored, 32 * i)
                nc.vector.tensor_tensor(z[0:H, :, cols], zhalf[1][0:H, 0:NLAYER:2, :], zother[0:H, 0:NLAYER:2, :],
                                        ALU.add)
                last = nc.vector.tensor_tensor(z[H:P, 0, cols], zhalf[1][H:P, 1, :], zother[H:P, 1, :], ALU.add)
                last.then_inc(z_ready, 1)

            dve.wait_ge(weights_in, 16 * 8)
            nc.vector.tensor_tensor(w0_sb[:, 0:L0_MT - 1, :], w0_sb[:, 0:L0_MT - 1, :],
                                    w0_swap_sb[:, 0:L0_MT - 1, :], ALU.add)
            nc.vector.tensor_tensor(w0_sb[0:P - M, L0_MT - 1, :], w0_sb[0:P - M, L0_MT - 1, :],
                                    w0_swap_sb[0:P - M, L0_MT - 1, :], ALU.add).then_inc(w0_summed, 1)
            layer0(0, 0)

            def tile(i, q):
                for p in range(2):
                    after = following(i, p)
                    layer12(i, p, 1, range(SUM_SLOT))
                    if is_int(2 * i + p, 0):
                        sum_over_d(0, 0, 0)
                    else:
                        sum_over_d(*((i - 1, 1) if p == 0 else (i, 0)), 2)
                    layer12(i, p, 1, range(SUM_SLOT, L12_SLOTS))
                    if exists(after[0]):
                        layer0(*after)
                    layer12(i, p, 2, range(SUM_SLOT))
                    if p == 0 and not is_int(i, 0):
                        add_chunks(i - 1)
                    sum_over_d(i, p, 1)
                    if exists(after[0]):
                        sum_over_d(*after, 0)
                    layer12(i, p, 2, range(SUM_SLOT, L12_SLOTS))

            all_turns(dve, tile)
            sum_over_d(TILES - 1, 1, 2)
            add_chunks(TILES - 1)

        @block.tensor
        def _(pe):
            def transpose(i, q, p):
                s = 2 * i + p
                if p == 0:
                    pe.wait_ge(gathered[q], gathered_count(i, q))
                if not is_int(s, 0):
                    pe.wait_ge(x0_ready, s)
                for c in range(2):
                    for d in range(DC):
                        last = nc.tensor.transpose(tr[0:M, c, P * d:P * (d + 1)],
                                                   emb[q][:, :, (2 * p + c) * DC + d], ident[:, :])
                last.then_inc(transposed, 1)

            def pair_tile(bank, weight, moving, start, stop):
                for c in range(2):
                    last = nc.tensor.matmul(bank[H * c:H * c + H, :], weight, moving[:, c, :],
                                            start=start, stop=stop)
                return last

            def take_bank(i, p, layer):
                run = run_of(i, p, layer)
                if not is_int(run, 0, 1):
                    pe.wait_ge(acc_used, run - 1)
                return acc[run_parity(i, p, layer)]

            def from_slots(i, p, layer, bank, weights, ks):
                for k in ks:
                    pe.wait_ge(slot_full, slot_of(i, p, layer, k) + 1)
                    first, width = slot_tiles(layer, k) if layer else (SLOT_MT * k, SLOT_MT)
                    for j in range(width):
                        last = pair_tile(bank, weights[:, first + j, :],
                                         slots[slot_buffer(i, p, layer, k)][:, :, j, :],
                                         start=layer > 0 and (k, j) == (0, 0),
                                         stop=first + j == weights.shape[1] - 1)
                    last.then_inc(slot_used, 1)

            def layer0(i, p):
                bank = take_bank(i, p, 0)
                pe.wait_ge(x0_ready, 2 * i + p + 1)
                pair_tile(bank, wd_sb[M * p:M * p + M, :],
                          squares[M * p:M * p + M, :].rearrange("p (c n) -> p c n", c=2), True, False)
                from_slots(i, p, 0, bank, w0_sb, range(L0_SLOTS))

            def layer12(i, p, layer, between=None):
                bank = take_bank(i, p, layer)
                weights = w12_sb[layer - 1]
                for k in range(L12_SLOTS):
                    if k == TR_SLOT and between:
                        transpose(*between)
                    if k == POOL_SLOT[layer]:
                        pe.wait_ge(pool_full, pool_run(i, p, layer) + 1)
                        for t in range(POOL_MT[layer]):
                            last = pair_tile(bank, weights[:, t, :], pool_prod[layer][:, :, t, :], False, False)
                        last.then_inc(pool_used, 1)
                    from_slots(i, p, layer, bank, weights, [k])

            pe.wait_ge(weights_in, 16 * 8)
            pe.wait_ge(ident_made, 2)
            pe.wait_ge(w0_summed, 1)
            transpose(0, 0, 0)
            transpose(0, 0, 1)
            layer0(0, 0)

            def mlp1(n, t, u):
                cols = slice(CH * n, CH * (n + 1))
                z = z_early[:, :, cols] if n < EARLY * P // CH else z_last
                if u >= 4:
                    pe.wait_ge(mlp_out, u - 3)
                nc.tensor.matmul(mlp_banks[u % 4], wt1[0][:, P * t:P * (t + 1)], z[:, 0, :],
                                 start=True, stop=False)
                nc.tensor.matmul(mlp_banks[u % 4], wt1[1][0:H + D, P * t:P * (t + 1)], z[0:H + D, 1, :],
                                 start=False, stop=True).then_inc(mlp_full, 1)

            def tile(i, q):
                for p in range(2):
                    after = following(i, p)
                    next_but_one = (i + 1, 1 - q, p) if exists(i + 1) else None
                    layer12(i, p, 1, between=next_but_one)
                    if exists(after[0]):
                        layer0(*after)
                    if is_int(2 * i + p, STEPS - 1):
                        pe.wait_ge(mlp_in, 16 * 8)
                        for t in range(2):
                            mlp1(0, t, t)
                    layer12(i, p, 2)

            all_turns(pe, tile)

            pe.wait_ge(acc_used, NLAYER * STEPS)
            for n in range(B // CH):
                if n == EARLY * P // CH:
                    pe.wait_ge(z_ready, TILES)
                for t in range(2 if n == 0 else 0, F1 // P):
                    mlp1(n, t, F1 // P * n + t)
            u = B // CH * (F1 // P)
            for n in range(B // CH):
                cols = slice(CH * n, CH * (n + 1))
                for t in range(F2 // P):
                    pe.wait_ge(mlp_out, max(u - 3, (n + 1) * (F1 // P)))
                    for q in range(F1 // P):
                        last = nc.tensor.matmul(mlp_banks[u % 4], wt2[:, q, P * t:P * (t + 1)], h1[:, q, cols],
                                                start=(q == 0), stop=(q == F1 // P - 1))
                    last.then_inc(mlp_full, 1)
                    u += 1
            pe.wait_ge(mlp_out, u)
            for q in range(F2 // P):
                for n in range(B // CH):
                    last = nc.tensor.matmul(mlp_banks[0][32 * n:32 * n + 1, :], wt3[:, q:q + 1],
                                            h2[:, q, CH * n:CH * (n + 1)], start=(q == 0), stop=(q == F2 // P - 1))
            last.then_inc(mlp_full, 1)

        @block.scalar
        def _(act):
            def take_x0(i, p):
                s = 2 * i + p
                act.wait_ge(transposed, s + 1)
                if not is_int(i, 0):
                    act.wait_ge(rep0_in[p], i * 16 * GROUP_DMAS)
                    for g in (1, 2, 3):
                        act.wait_ge(rep_in[g], (s - 1) * 16 * GROUP_DMAS)
                for g in range(P // M):
                    copy = nc.scalar.activation(x0t[p][M * g:M * g + M, :].rearrange("p (c n) -> p c n", c=2),
                                                tr[0:M, :, :], ACT.Copy)
                    if g == 1 and is_int(s, 0):
                        copy.then_inc(x0_halfway, 1)
                nc.scalar.activation(squares[M * p:M * p + M, :].rearrange("p (c n) -> p c n", c=2), tr[0:M, :, :],
                                     ACT.Square).then_inc(x0_ready, 1)

            def finish(i, p, layer):
                run = run_of(i, p, layer)
                bank = acc[run_parity(i, p, layer)]
                act.wait_ge(slot_used, slot_of(i, p, layer) + (L12_SLOTS if layer else L0_SLOTS))
                def both_halves(x, c):
                    for half in range(2):
                        last = nc.scalar.activation(x[H * half:H * half + H, c, :],
                                                    bank[H * c:H * c + H, :], ACT.Relu)
                    return last

                if layer < 2:
                    for c in range(2):
                        both_halves(x_ps[p], c).then_inc(x_ready, 1)
                    if layer == 1:
                        act.wait_ge(pool_full, pool_run(i, p, 1) + 1)
                    elif not is_int(i, 0):
                        act.wait_ge(pool_full, pool_run(i - 1, p, 2) + 1)
                    both_halves(x_pool[p], 0)
                    both_halves(x_pool[p], 1).then_inc(x_pool_ready, 1)
                if not is_int(run, 0, 1):
                    act.wait_ge(summed, run - 1)
                nc.scalar.activation(stacked[run_parity(i, p, layer)][:, :], bank[:, :], ACT.Relu)\
                    .then_inc(acc_used, 1)

            take_x0(0, 0)
            take_x0(0, 1)
            finish(0, 0, 0)

            def swap_chunks(i):
                act.wait_ge(z_summed, i + 1)
                nc.scalar.activation(zother[0:H, 0:NLAYER:2, :], zhalf[1][H:P, 0:NLAYER:2, :], ACT.Copy)
                nc.scalar.activation(zother[H:P, 1, :], zhalf[1][0:H, 1, :], ACT.Copy).then_inc(z_moved, 1)

            def tile(i, q):
                for p in range(2):
                    after = following(i, p)
                    if p == 0 and not is_int(i, 0):
                        swap_chunks(i - 1)
                    if exists(i + 1):
                        take_x0(i + 1, p)
                    finish(i, p, 1)
                    if exists(after[0]):
                        finish(*after, 0)
                    finish(i, p, 2)

            all_turns(act, tile)

            swap_chunks(TILES - 1)
            act.wait_ge(weights_in, 16 * 8)
            act.wait_ge(slot_full, slot_of(TILES - 1, 1, 2) + L12_SLOTS)
            act.wait_ge(pool_full, pool_run(TILES - 1, 1, 2) + 1)
            u = 0
            for bias, hidden, width in ((b1_sb, h1, F1), (b2_sb, h2, F2)):
                for n in range(B // CH):
                    for t in range(width // P):
                        act.wait_ge(mlp_full, u + 1)
                        nc.scalar.activation(hidden[:, t, CH * n:CH * (n + 1)], mlp_banks[u % 4], ACT.Relu,
                                             bias=bias[:, t:t + 1]).then_inc(mlp_out, 1)
                        u += 1
            act.wait_ge(mlp_full, u + 1)
            for n in range(B // CH):
                last = nc.scalar.activation(y_sb[32 * n:32 * n + 1, :], mlp_banks[0][32 * n:32 * n + 1, :], ACT.Copy)
            last.then_inc(mlp_out, 1)


def kernel(**inputs):
    import numpy as np
    import concourse.bacc as bacc
    from concourse import mybir as mb
    from concourse.bass_utils import run_bass_kernel_spmd

    w0 = np.asarray(inputs["L0_rec_W0"])
    m = np.arange(M)[None, :, None]
    shift = (np.arange(P // M)[:, None, None] + 1) + P // M * np.arange(L0_MT)[None, None, :]
    h = (m + shift) % M
    m = np.broadcast_to(m, h.shape)
    named = {
        "dense_t": np.ascontiguousarray(np.asarray(inputs["dense_ctx"]).T),
        "ids": np.ascontiguousarray(inputs["ids"]),
        **{f"tbl_{n}": np.ascontiguousarray(inputs[f"tbl_{n}"]) for n in range(M)},
        **{k: np.ascontiguousarray(inputs[k]) for k in ("W_top1", "b_top1", "W_top2", "b_top2", "W_top3")},
        "w0_pair": np.ascontiguousarray(w0[m, h].reshape(P, L0_MT, H)),
        "w0_swap": np.ascontiguousarray(w0[h, m].reshape(P, L0_MT, H)),
        "w0_diag": np.ascontiguousarray(w0[np.arange(M), np.arange(M)]),
        "W1": np.ascontiguousarray(inputs["L0_rec_W1"]),
        "W2": np.ascontiguousarray(inputs["L0_rec_W2"]),
    }
    nc = bacc.Bacc("TRN2", target_bir_lowering=False, num_devices=1)
    args = {k: nc.dram_tensor(f"in_{k}", a.shape, mb.dt.from_np(a.dtype), kind="ExternalInput").ap()
            for k, a in named.items()}
    z_dram = nc.dram_tensor("z_dram", (2, P, P * EARLY), mb.dt.float32, kind="Internal").ap()
    out = nc.dram_tensor("out_y", (B, 1), mb.dt.float32, kind="ExternalOutput").ap()
    cin(nc, args["dense_t"], args["ids"], [args[f"tbl_{n}"] for n in range(M)], args["W_top1"],
        args["b_top1"], args["W_top2"], args["b_top2"], args["W_top3"], args["w0_pair"], args["w0_swap"],
        args["w0_diag"], args["W1"], args["W2"], z_dram, out)
    r = run_bass_kernel_spmd(nc, [{f"in_{k}": a for k, a in named.items()}], core_ids=[0])
    return r.results[0]["out_y"]
```
